# Optimizing a Trainium2 kernel written in Bass

```python
import numpy as np
import jax
import jax.numpy as jnp

def _softmax(x, axis=-1):
    return jax.nn.softmax(x, axis=axis)

def _gelu(x):
    return jax.nn.gelu(x, approximate=True)

def _silu(x):
    return jax.nn.silu(x)

def _sigmoid(x):
    return jax.nn.sigmoid(x)

def _layernorm(x, axis=-1, eps=1e-05):
    m = jnp.mean(x, axis=axis, keepdims=True)
    v = jnp.var(x, axis=axis, keepdims=True)
    return (x - m) / jnp.sqrt(v + eps)

def _scatter_add(tgt, idx, src, axis=0):
    return tgt.at[idx].add(src)

def _segment_sum(src, seg, n):
    return jax.ops.segment_sum(src, seg, n)
kernel_name = 'mk_metaformer_d1_conv_nchw128_r2_545e35'

def setup_inputs(seed: int=0):
    np.random.seed(seed)
    _w = jnp.asarray

    def _rec_inputs():
        import jax
        import jax.numpy as jnp
        _gk = jax.random.key(seed)
        x = -0.000125 + 0.9999 * jax.random.normal(jax.random.fold_in(_gk, 1), (4, 64, 128, 128), jnp.float32)
        return x
    x = _rec_inputs()

    def _L0_conv_setup():
        import jax, jax.numpy as jnp
        import numpy as np

        def _conv1x1(x, W, b):
            return jnp.einsum('oc,bchw->bohw', W, x) + b[None, :, None, None]
        key = jax.random.key(seed)
        ks = jax.random.split(key, 9)
        B, Cin, H, W = (4, 64, 128, 128)
        Ck, Cv = (64, 64)
        s = 0.02
        return {'x': jax.random.normal(ks[0], (B, Cin, H, W), dtype=jnp.float32), 'Wk': jax.random.normal(ks[1], (Ck, Cin), dtype=jnp.float32) * s, 'bk': jax.random.normal(ks[2], (Ck,), dtype=jnp.float32) * s, 'Wq': jax.random.normal(ks[3], (Ck, Cin), dtype=jnp.float32) * s, 'bq': jax.random.normal(ks[4], (Ck,), dtype=jnp.float32) * s, 'Wv': jax.random.normal(ks[5], (Cv, Cin), dtype=jnp.float32) * s, 'bv': jax.random.normal(ks[6], (Cv,), dtype=jnp.float32) * s, 'Wr': jax.random.normal(ks[7], (Cin, Cv), dtype=jnp.float32) * s, 'br': jax.random.normal(ks[8], (Cin,), dtype=jnp.float32) * s, 'head_count': 8}
    _L0_conv_all = _L0_conv_setup()
    _L0_conv_in = {k: v for k, v in _L0_conv_all.items() if k in ('Wk', 'bk', 'Wq', 'bq', 'Wv', 'bv', 'Wr', 'br')}
    del _L0_conv_all

    def _L0_ffn_setup():
        import jax, jax.numpy as jnp
        import numpy as np
        B, N, D, C, E, K = (8, 4096, 64, 64, 8, 2)
        key = jax.random.key(seed)
        k0, k1, k2 = jax.random.split(key, 3)
        x = jax.random.normal(k0, (B, N, D), dtype=jnp.float32)
        router_w = jax.random.normal(k1, (D, E), dtype=jnp.float32) * 0.05
        router_b = jnp.zeros((E,), dtype=jnp.float32)
        expert_w = jax.random.normal(k2, (E, D, C), dtype=jnp.float32) * (1.0 / np.sqrt(D))
        expert_b = jnp.zeros((E, C), dtype=jnp.float32)
        return {'x': x, 'router_w': router_w, 'router_b': router_b, 'expert_w': expert_w, 'expert_b': expert_b}
    _L0_ffn_all = _L0_ffn_setup()
    _L0_ffn_in = {k: v for k, v in _L0_ffn_all.items() if k in ('router_w', 'router_b', 'expert_w', 'expert_b')}
    del _L0_ffn_all
    return {'x': x, 'L0_conv_Wk': _L0_conv_in['Wk'], 'L0_conv_bk': _L0_conv_in['bk'], 'L0_conv_Wq': _L0_conv_in['Wq'], 'L0_conv_bq': _L0_conv_in['bq'], 'L0_conv_Wv': _L0_conv_in['Wv'], 'L0_conv_bv': _L0_conv_in['bv'], 'L0_conv_Wr': _L0_conv_in['Wr'], 'L0_conv_br': _L0_conv_in['br'], 'L0_ffn_router_w': _L0_ffn_in['router_w'], 'L0_ffn_router_b': _L0_ffn_in['router_b'], 'L0_ffn_expert_w': _L0_ffn_in['expert_w'], 'L0_ffn_expert_b': _L0_ffn_in['expert_b']}

def reference(x, L0_conv_Wk, L0_conv_bk, L0_conv_Wq, L0_conv_bq, L0_conv_Wv, L0_conv_bv, L0_conv_Wr, L0_conv_br, L0_ffn_router_w, L0_ffn_router_b, L0_ffn_expert_w, L0_ffn_expert_b):
    import jax
    import jax.numpy as jnp

    def _L0_conv_ref(x, Wk, bk, Wq, bq, Wv, bv, Wr, br, head_count):
        import jax, jax.numpy as jnp
        import numpy as np

        def _conv1x1(x, W, b):
            return jnp.einsum('oc,bchw->bohw', W, x) + b[None, :, None, None]
        B, Cin, H, W = x.shape
        N = H * W
        Ck = Wk.shape[0]
        Cv = Wv.shape[0]
        hk = Ck // head_count
        hv = Cv // head_count
        k = jax.nn.relu(_conv1x1(x, Wk, bk).reshape(B, head_count, hk, N))
        q = jax.nn.relu(_conv1x1(x, Wq, bq).reshape(B, head_count, hk, N))
        v = _conv1x1(x, Wv, bv).reshape(B, head_count, hv, N)
        context = jnp.einsum('bhkn,bhvn->bhkv', k, v)
        attended = jnp.einsum('bhkv,bhkn->bhvn', context, q)
        agg = attended.reshape(B, Cv, H, W)
        return _conv1x1(agg, Wr, br)

    def _L0_ffn_ref(x, router_w, router_b, expert_w, expert_b):
        import jax, jax.numpy as jnp
        import numpy as np
        B, N, D, C, E, K = (8, 4096, 64, 64, 8, 2)
        router_probs = jax.nn.softmax(x @ router_w + router_b, axis=-1)
        top_p, top_i = jax.lax.top_k(router_probs, K)
        top_p = top_p / jnp.sum(top_p, axis=-1, keepdims=True)
        expert_out = jnp.einsum('bnd,edc->bnec', x, expert_w) + expert_b
        gathered = jnp.take_along_axis(expert_out, top_i[..., None], axis=2)
        return jnp.einsum('bnk,bnkc->bnc', top_p, gathered)

    def _gn(v, G=32, eps=1e-05):
        B_, C_, H_, W_ = v.shape
        g = v.reshape(B_, G, C_ // G, H_, W_)
        m = jnp.mean(g, axis=(2, 3, 4), keepdims=True)
        s = jnp.var(g, axis=(2, 3, 4), keepdims=True)
        return ((g - m) / jnp.sqrt(s + eps)).reshape(v.shape)

    def _ln_c(v, eps=1e-06):
        m = jnp.mean(v, axis=1, keepdims=True)
        s = jnp.var(v, axis=1, keepdims=True)
        return (v - m) / jnp.sqrt(s + eps)

    def _ln_t(v, eps=1e-05):
        m = jnp.mean(v, axis=-1, keepdims=True)
        s = jnp.var(v, axis=-1, keepdims=True)
        return (v - m) / jnp.sqrt(s + eps)

    def _to_tokens(v):
        B_, C_, H_, W_ = v.shape
        return v.reshape(B_, C_, H_ * W_).transpose(0, 2, 1)

    def _from_tokens(t, like):
        B_, C_, H_, W_ = like.shape
        return t.transpose(0, 2, 1).reshape(B_, C_, H_, W_)
    x = x + _L0_conv_ref(_ln_c(x), L0_conv_Wk, L0_conv_bk, L0_conv_Wq, L0_conv_bq, L0_conv_Wv, L0_conv_bv, L0_conv_Wr, L0_conv_br, 8)
    t = _to_tokens(x)
    t = t + _L0_ffn_ref(_ln_t(t), L0_ffn_router_w, L0_ffn_router_b, L0_ffn_expert_w, L0_ffn_expert_b)
    x = _from_tokens(t, x)
    return x

_drawn_inputs = setup_inputs


def setup_inputs(seed=0):
    import zlib

    import numpy as np

    out = dict(_drawn_inputs(seed))
    spreads = {'L0_ffn_router_b': (0.0, 0.1), 'L0_ffn_expert_b': (0.0, 0.295)}
    factors = {'L0_conv_br': 3.255}
    for name, (base, spread) in spreads.items():
        noise = np.random.default_rng([zlib.crc32(name.encode()), seed]).standard_normal(out[name].shape)
        drawn = base * np.exp(spread * noise) if base else spread * noise
        out[name] = jnp.asarray(drawn.astype(out[name].dtype))
    for name, factor in factors.items():
        out[name] = (out[name] * factor).astype(out[name].dtype)
    return out
```

```python
from contextlib import ExitStack

import numpy as np

import concourse.bass as bass
from concourse import mybir

ALU = mybir.AluOpType
ACT = mybir.ActivationFunctionType
AX_X = mybir.AxisListType.X
F32 = mybir.dt.float32
F16 = mybir.dt.float16
BF16 = mybir.dt.bfloat16

P = 128
BATCH, C, HW = 4, 64, 128 * 128
HEADS = 8
E = 8
S = 2
NT = 512
NJ = NT // P
TPB = HW // (S * NT)
TILES = BATCH * TPB
GR = NJ * S
SE = S * E
CHUNKS = E // 2 * S
KIND = 8
LO = 2.0 ** -11
EPS_CONV, EPS_FFN = 1e-6, 1e-5
BIG = 1e30
PG = 2 * GR
AHEAD = 3
NLG = SE + S


def constants():
    eye = np.eye(P, dtype=np.float32)
    half = np.arange(P) // C
    same = (half[:, None] == half[None, :]).astype(np.float32)
    centre = eye - same / C
    ch = np.arange(P) % C
    heads = (ch[:, None] // (C // HEADS) == np.arange(C)[None, :] // (C // HEADS)).astype(np.float32)
    kind, row_s, row_e = np.arange(P) // SE, np.arange(P) // E % S, np.arange(P) % E
    parts = np.zeros((P, 3), np.float32)
    for j in range(3):
        parts[kind == 2 + j, j] = 1.0
        parts[kind == 5 + j, j] = LO
    first = np.broadcast_to(np.arange(E, 0, -1, dtype=np.float32), (P, E))
    means = np.zeros((P, S), np.float32)
    for s in range(S):
        means[half == s, s] = 1.0 / C
    f32 = np.concatenate([eye, centre, same, heads, parts, first, means], axis=1)
    sel = np.zeros((P, CHUNKS, P), np.float16)
    for p in range(E // 2):
        for s in range(S):
            for m in range(P):
                hit = (row_s == s) & (row_e == 2 * p + m // C)
                sel[hit & (kind == 0), p * S + s, m] = 1.0
                sel[hit & (kind == 1), p * S + s, m] = LO
    return np.ascontiguousarray(f32), sel.reshape(P, CHUNKS * P), np.eye(P, dtype=np.float16)


def metaformer_block(nc, x, Wk, bk, Wq, bq, Wv, bv, Wr, br, router_w, router_b, expert_w, expert_b,
                     const32, const_sel, const_eye, out):
    x_t = x.rearrange("b c h w -> b c (h w)").rearrange("b c (s i n) -> b s c i n", s=S, n=NT)
    o_t = out.rearrange("b c h w -> b c (h w)").rearrange("b c (s i n) -> b s c i n", s=S, n=NT)

    with ExitStack() as ctx:
        def sb(name, shape, dt=F32):
            return ctx.enter_context(nc.sbuf_tensor(name, shape, dt))

        def sem(name):
            return ctx.enter_context(nc.semaphore(name))

        k32 = sb("k32", [P, 3 * P + C + 3 + E + S])
        eye = k32[:, 0:P]
        centre = k32[:, P:2 * P]
        same_half = k32[:, 2 * P:3 * P]
        same_head = k32[:, 3 * P:3 * P + C]
        part_scale = k32[:, 3 * P + C:3 * P + C + 3]
        first_wins = k32[:, 3 * P + C + 3:3 * P + C + 3 + E]
        half_mean = k32[:, 3 * P + C + 3 + E:3 * P + C + 3 + E + S]
        sel = sb("sel", [P, CHUNKS, P], F16)
        eye16 = sb("eye16", [P, P], F16)
        w_nat = sb("w_nat", [P, 4, P])
        w_cen = sb("w_cen", [P, 3, P])
        w_mean = sb("w_mean", [P, 3])
        wk_bd = sb("wk_bd", [P, P])
        wq_bd = sb("wq_bd", [P, P])
        wvT = sb("wvT", [P, C])
        wrT = sb("wrT", [P, C])
        bk_row = sb("bk_row", [1, 4, C])
        bk_part = sb("bk_part", [1, 2, C], BF16)
        bk_rows = sb("bk_rows", [P, NT // C, C], BF16)
        ones16 = sb("ones16", [P, P], BF16)
        zeros16 = sb("zeros16", [P, P + 1], BF16)
        bq_col = sb("bq_col", [P, 1])
        br_col = sb("br_col", [P, 1])
        bv_row = sb("bv_row", [P, C])
        rb_row = sb("rb_row", [P, E])
        rw_nat = sb("rw_nat", [P, P])
        rw_bd = sb("rw_bd", [P, P])
        ew_nat = sb("ew_nat", [P, E // 2, C])
        ew = sb("ew", [P, E // 2, C])
        eb_nat = sb("eb_nat", [P, P])
        eb_left = sb("eb_left", [P, 2, P])
        eb_part = sb("eb_part", [P, 3, P], BF16)
        eb_rows = sb("eb_rows", [P, P], BF16)

        xin = sb("xin", [P, 2, NT])
        xT = sb("xT", [P, 2, NT])
        sq = sb("sq", [P, 2, NT])
        stat = sb("stat", [P, 6, GR])
        xnT = sb("xnT", [P, 2, NJ, P + 1])
        xn = sb("xn", [P, 2, NT])
        keys = sb("keys", [P, 2, NT])
        kept = sb("kept", [P, TPB * NT])
        minus_half = sb("minus_half", [P, 1])
        one16 = sb("one16", [P, SE], F16)
        assert SE == PG
        s_sb = sb("s_sb", [P, P + 1])
        sT_sb = sb("sT_sb", [P, P])
        ctx_sb = sb("ctx_sb", [P, 2, C])
        ctxT_sb = sb("ctxT_sb", [C, 3, C])
        att = sb("att", [P, P])

        x1 = sb("x1", [P, 2, NT])
        lg = sb("lg", [P, TPB * NJ, NLG])
        ssq = sb("ssq", [P, TPB, GR])

        bstat = sb("bstat", [P, 4, TPB * GR])
        gstat = sb("gstat", [P, 5, PG])
        grstd = sb("grstd", [P, PG])
        gl = sb("gl", [P, PG, E])
        gd = sb("gd", [P, 2, PG, E])
        gex = sb("gex", [P, PG, E])
        gk = sb("gk", [P, 2, PG, E])
        g2 = sb("g2", [P, 2 * NJ, 2, SE])
        g2h = sb("g2h", [P, 2 * NJ, 2, SE], F16)
        gT = sb("gT", [P, 2 * NJ, P], F16)

        x1d = sb("x1d", [P, 2, S, NT])
        grows = sb("grows", [P, 2, NT], F16)
        gbs = sb("gbs", [P, 3, NT])
        z = sb("z", [P, 4, NT])
        osb = sb("osb", [P, 2, NT])

        bank = [ctx.enter_context(nc.psum_tensor(f"bank{i}", [P, NT], F32)) for i in range(8)]
        bA, bB, bC, bD, bE, bF, bG, bH = bank
        attn_bank = [bB, bD]
        gb_bank = [bC, bE, bF, bG]
        gT_bank = [bB, bD]
        out_bank = [bH, bA]

        const_in = sem("const_in")
        cleared = sem("cleared")
        weights_in = sem("weights_in")
        set_dve = sem("set_dve")
        set_pe = sem("set_pe")
        x_in = [sem(f"x_in{i}") for i in range(2)]
        xT_ready = sem("xT_ready")
        xT_copied = sem("xT_copied")
        xT_squared = sem("xT_squared")
        stat_own = sem("stat_own")
        norm_own = sem("norm_own")
        pool_own = sem("pool_own")
        norm_done = sem("norm_done")
        xn_ready = sem("xn_ready")
        xn_copied = sem("xn_copied")
        k_ready = sem("k_ready")
        k_done = sem("k_done")
        q_ready = sem("q_ready")
        q_done = sem("q_done")
        sum_done = sem("sum_done")
        fin_pe = sem("fin_pe")
        fin_dve = sem("fin_dve")
        attn_ready = sem("attn_ready")
        x1_done = sem("x1_done")
        x1_kept = sem("x1_kept")
        x1T_ready = sem("x1T_ready")
        x1_squared = sem("x1_squared")
        lg_ready = sem("lg_ready")
        lg_copied = sem("lg_copied")
        ssq_done = sem("ssq_done")
        dev_done = sem("dev_done")
        gate_dve = sem("gate_dve")
        gate_pool = sem("gate_pool")
        exp_done = sem("exp_done")
        x1d_in = [sem(f"x1d_in{i}") for i in range(2)]
        gT_ready = sem("gT_ready")
        grows_done = sem("grows_done")
        gb_ready = sem("gb_ready")
        gb_copied = sem("gb_copied")
        z_dve = sem("z_dve")
        z_pool = sem("z_pool")
        prod_done = sem("prod_done")
        out_done = sem("out_done")
        stored = [sem(f"stored{i}") for i in range(2)]

        BY_POOL = (2, 4, 7)
        ND, NP = CHUNKS - len(BY_POOL), len(BY_POOL)
        BY_DVE = [c for c in range(CHUNKS) if c not in BY_POOL]
        credit = {norm_done: 2, sum_done: 2, q_ready: 2, lg_ready: 2, x1_kept: 2, x1_done: 2, ssq_done: 2,
                  out_done: 2, grows_done: 2, xT_squared: 1, xn_copied: 1, k_done: 1, q_done: 1, x1_squared: 1,
                  lg_copied: 1, gT_ready: 1, stored[0]: 16, stored[1]: 16,
                  z_dve: ND, gb_copied: NP, z_pool: NP, prod_done: 4}
        credit = {s.name: n for s, n in credit.items()}
        N_FIN_PE, N_FIN_DVE, N_STAT, N_DEV = 4, 9, 5, 3
        N_GATE_DVE, N_GATE_POOL = 16, 10
        N_SET_CEN, N_SET_DVE = 14, 36
        N_LOADS = S * (7 + KIND - 2) + 4

        def done(eng, signal, n, more=0):
            eng.wait_ge(signal, n + (more + credit.get(signal.name, 0)))

        def give_credit(eng, *signals):
            for s in signals:
                eng.sem_inc(s, credit[s.name])

        def wait_product(eng, t, c):
            if c in BY_POOL:
                done(eng, z_pool, t * NP, BY_POOL.index(c) + 1)
            else:
                done(eng, z_dve, t * ND, BY_DVE.index(c) + 1)

        def wait_gates_read(eng, t, c):
            k, back = c % CHUNKS, c < 0
            if k in BY_POOL:
                done(eng, gb_copied, t * NP, BY_POOL.index(k) + 1 - back * NP)
            else:
                done(eng, z_dve, t * ND, BY_DVE.index(k) + 1 - back * ND)

        block = ctx.enter_context(nc.Block())

        @block.sync
        def _(sp):
            count = [0]

            def load(dst, src):
                sp.dma_start(dst, src).then_inc(weights_in, 16)
                count[0] += 1

            def load_x(b, i, u):
                for s in range(S):
                    sp.dma_start(xin[C * s:C * s + C, u, :], x_t[b, s, :, i, :]).then_inc(x_in[u], 16)

            def spread(i, u):
                for s in range(S):
                    for d in range(2):
                        sp.dma_start(x1d[C * d:C * d + C, u, s, :],
                                     kept[C * s:C * s + C, bass.ds(i * NT, NT)]).then_inc(x1d_in[u], 16)

            def store(b, i, u):
                for s in range(S):
                    sp.dma_start(o_t[b, s, :, i, :], osb[C * s:C * s + C, u, :]).then_inc(stored[u], 16)

            give_credit(sp, *stored)
            sp.dma_start(k32[:, :], const32).then_inc(const_in, 16)
            sp.dma_start(sel[:, :, :].rearrange("p a b -> p (a b)"), const_sel).then_inc(const_in, 16)
            sp.dma_start(eye16[:, :], const_eye).then_inc(const_in, 16)
            sp.wait_ge(cleared, 3)
            for s in range(S):
                rows = slice(C * s, C * s + C)
                load(w_nat[rows, 0, rows], Wk)
                load(w_nat[rows, 1, rows], Wq)
                load(w_nat[0:C, 2, rows], Wv)
                load(bq_col[rows, :], bq.rearrange("(c a) -> c a", a=1))
                load(br_col[rows, :], br.rearrange("(c a) -> c a", a=1))
                load(rw_nat[rows, E * s:E * s + E], router_w)
                load(ew_nat[rows, :, :], expert_w.rearrange("(p a) d c -> a d p c", a=2)[s])
                for kind in range(2, KIND):
                    r = kind * SE + s * E
                    load(eb_nat[r:r + E, rows], expert_b)
            load(w_nat[0:C, 3, 0:C], Wr)
            load(bk_row[0:1, 0, :], bk.rearrange("(a c) -> a c", a=1))
            load(bv_row[:, :], bv.rearrange("(a c) -> a c", a=1).to_broadcast([P, C]))
            load(rb_row[:, :], router_b.rearrange("(a c) -> a c", a=1).to_broadcast([P, E]))
            assert count[0] == N_LOADS

            with sp.Fori(0, BATCH) as b:
                for u in range(2):
                    load_x(b, u, u)
                with sp.Fori(0, TPB // 2 - 1) as pair:
                    i = 2 * pair
                    for u in range(2):
                        done(sp, xT_ready, b * TPB + i + u + 1)
                        load_x(b, i + u + 2, u)
                for u in range(2):
                    done(sp, xT_ready, b * TPB + TPB - 1 + u)
                    load_x(b, u, u)
                with sp.Fori(0, TPB // 2 - 1) as pair:
                    i = 2 * pair
                    for u in range(2):
                        done(sp, x1_done, b * TPB + i + u + 1)
                        load_x(b, i + u + 2, u)
                done(sp, x1_kept, b * TPB + TPB)
                for u in range(2):
                    spread(u, u)
                with sp.Fori(0, TPB // 2 - 1) as pair:
                    i = 2 * pair
                    for u in range(2):
                        t = b * TPB + i + u
                        wait_product(sp, t, BY_DVE[-1])
                        wait_product(sp, t, BY_POOL[-1])
                        spread(i + u + 2, u)
                        done(sp, out_done, t + 1)
                        store(b, i + u, u)
                for u in range(2):
                    done(sp, out_done, b * TPB + TPB - 1 + u)
                    store(b, TPB - 2 + u, u)
            for u in range(2):
                done(sp, stored[u], 16 * S * TILES // 2)

        def over_experts(a):
            return a.unsqueeze(2).to_broadcast([P, PG, E])

        def by_half(a):
            return a.rearrange("p (a s) e -> p a s e", s=S)

        @block.gpsimd
        def _(pool):
            for tile in (w_nat, rw_nat, eb_nat):
                pool.memset(tile[:], 0.0).then_inc(cleared, 1)
            give_credit(pool, z_pool)
            pool.wait_ge(weights_in, 16 * N_LOADS)
            pool.wait_ge(const_in, 16 * 3)

            def gate_steps(b, h):
                n = b * (TPB // 2) + h
                dve, own = n * N_GATE_DVE, n * N_GATE_POOL
                i = 2 * h
                kinds = g2[:, :, :, :].rearrange("p a k (s e) -> p a k s e", s=S)

                def pick():
                    pool.tensor_tensor(grstd[:, :], bstat[:, 3, bass.ds(i * GR, PG)],
                                       one16[:, :], ALU.mult).then_inc(gate_pool, 1)

                def scale():
                    pool.wait_ge(gate_pool, own + 1)
                    pool.tensor_tensor(by_half(gl[:, :, :]),
                                       lg[:, bass.ds(i * NJ, 2 * NJ), 0:SE].rearrange("p a (s e) -> p a s e", s=S),
                                       by_half(over_experts(grstd[:, :])), ALU.mult).then_inc(gate_pool, 1)

                def bias():
                    pool.wait_ge(gate_pool, own + 2)
                    pool.tensor_tensor(gl[:, :, :], gl[:, :, :],
                                       rb_row[:, :].unsqueeze(1).to_broadcast([P, PG, E]),
                                       ALU.add).then_inc(gate_pool, 1)

                def below_top():
                    pool.wait_ge(gate_dve, dve + 1)
                    pool.tensor_tensor(gd[:, 0], gl[:, :, :], over_experts(gstat[:, 0, :]),
                                       ALU.subtract).then_inc(gate_pool, 1)

                def choose():
                    pool.wait_ge(gate_dve, dve + 11)
                    pool.wait_ge(exp_done, n + 1)
                    pool.tensor_tensor(gl[:, :, :], gex[:, :, :], gk[:, 0], ALU.mult).then_inc(gate_pool, 1)

                def gate():
                    pool.wait_ge(gate_dve, dve + 13)
                    pool.tensor_tensor(kinds[:, :, 1], by_half(gl[:, :, :]), by_half(over_experts(gstat[:, 4, :])),
                                       ALU.mult).then_inc(gate_pool, 1)

                def gate_over_dev():
                    pool.wait_ge(gate_pool, own + 6)
                    pool.tensor_tensor(kinds[:, :, 0], kinds[:, :, 1], by_half(over_experts(grstd[:, :])),
                                       ALU.mult).then_inc(gate_pool, 1)

                def left():
                    pool.wait_ge(gate_dve, dve + 14)
                    pool.tensor_tensor(g2[:, :, :, :], g2[:, :, :, :], g2h[:, :, :, :],
                                       ALU.subtract).then_inc(gate_pool, 1)

                def rows_scaled():
                    done(pool, gT_ready, b * TPB + i)
                    pool.tensor_tensor(gT[:, :, 0:SE], g2h[:, :, 0, :],
                                       one16[:, :].unsqueeze(1).to_broadcast([P, 2 * NJ, SE]),
                                       ALU.mult).then_inc(gate_pool, 1)

                def rows_plain():
                    pool.tensor_copy(gT[:, :, 2 * SE:5 * SE].rearrange("p a (k r) -> p a k r", k=3),
                                     g2h[:, :, 1, :].unsqueeze(2).to_broadcast([P, 2 * NJ, 3, SE])
                                     ).then_inc(gate_pool, 1)

                steps = [pick, scale, bias, below_top, choose, gate, gate_over_dev, left, rows_scaled, rows_plain]
                assert len(steps) == N_GATE_POOL
                return steps

            def products(b, i, u, between):
                t = b * TPB + i + u
                pool.wait_ge(x1d_in[u], b * (32 * TPB) + i * 32 + 64)
                for k, c in enumerate(BY_POOL):
                    done(pool, gb_copied, t * NP + k + 1)
                    done(pool, prod_done, t * CHUNKS, c - 3)
                    pool.tensor_tensor(z[:, c % 4, :], gbs[:, k, :], x1d[:, u, c % S, :],
                                       ALU.mult).then_inc(z_pool, 1)
                    for step in between[k]:
                        step()

            pool.memset(minus_half[:, :], -0.5).then_inc(pool_own, 1)
            pool.memset(one16[:, :], 1.0).then_inc(pool_own, 1)
            pool.wait_ge(pool_own, 2)
            with pool.Fori(0, BATCH) as b:
                with pool.Fori(0, TPB) as i:
                    t = b * TPB + i
                    pool.wait_ge(stat_own, t * N_STAT + N_STAT)
                    done(pool, norm_done, t)
                    pool.tensor_tensor(stat[:, 5, :], stat[:, 4, :], minus_half[:, :].to_broadcast([P, GR]),
                                       ALU.pow).then_inc(norm_own, 1)
                pool.wait_ge(dev_done, b * N_DEV + N_DEV)
                pool.tensor_tensor(bstat[:, 3, :], bstat[:, 2, :], minus_half[:, :].to_broadcast([P, TPB * GR]),
                                   ALU.pow).then_inc(pool_own, 1)
                pool.wait_ge(pool_own, b + 3)
                for step in gate_steps(b, 0):
                    step()
                with pool.Fori(0, TPB // 2 - 1) as pair:
                    i = 2 * pair
                    g = gate_steps(b, pair + 1)
                    for step in g[0:3]:
                        step()
                    products(b, i, 0, [[g[3]], [], []])
                    g[4]()
                    products(b, i, 1, [[g[5], g[6]], [g[7], g[8], g[9]], []])
                for u in range(2):
                    products(b, TPB - 2, u, [[], [], []])

        @block.scalar
        def _(act):
            give_credit(act, x1_kept, grows_done, gb_copied, xT_squared, xn_copied, k_done, q_done, x1_squared)
            act.wait_ge(weights_in, 16 * N_LOADS)

            def spread_rows(t, u):
                done(act, gT_ready, t + 1)
                nc.scalar.copy(grows[:, u, :], gT_bank[u][:, 0:NT // 2].bitcast(F16)).then_inc(grows_done, 1)

            with act.Fori(0, BATCH) as b:
                def take_x(t, u):
                    act.wait_ge(xT_ready, t + 1)
                    done(act, norm_done, t, -1)
                    nc.scalar.copy(xT[:, u, :], bA[:, :]).then_inc(xT_copied, 1)
                    nc.scalar.activation(sq[:, u, :], bA[:, :], ACT.Square, scale=C ** -0.5).then_inc(xT_squared, 1)

                def take_xn(t, u):
                    act.wait_ge(xn_ready, t + 1)
                    done(act, q_ready, t, -1)
                    nc.scalar.copy(xn[:, u, :], bB[:, :]).then_inc(xn_copied, 1)

                def take_kq(t, u, i):
                    act.wait_ge(k_ready, t + 1)
                    done(act, sum_done, t, -1)
                    nc.scalar.activation(keys[:, u, :], bC[:, :], ACT.Relu).then_inc(k_done, 1)
                    done(act, q_ready, t + 1)
                    nc.scalar.activation(kept[:, bass.ds(i * NT, NT)], bD[:, :], ACT.Relu,
                                         bias=bq_col[:, 0:1]).then_inc(q_done, 1)

                t0 = b * TPB
                take_x(t0, 0)
                take_x(t0 + 1, 1)
                take_xn(t0, 0)
                with act.Fori(0, TPB // 2 - 1) as pair:
                    i = 2 * pair
                    for u in range(2):
                        take_kq(t0 + i + u, u, i + u)
                        take_x(t0 + i + u + 2, u)
                        take_xn(t0 + i + u + 1, 1 - u)
                take_kq(t0 + TPB - 2, 0, TPB - 2)
                take_xn(t0 + TPB - 1, 1)
                take_kq(t0 + TPB - 1, 1, TPB - 1)

                with act.Fori(0, TPB // 2) as pair:
                    i = 2 * pair
                    for u in range(2):
                        t = t0 + i + u
                        done(act, x1_done, t + 1)
                        done(act, attn_ready, t + 1)
                        nc.scalar.copy(kept[:, bass.ds((i + u) * NT, NT)], x1[:, u, :]).then_inc(x1_kept, 1)
                        act.wait_ge(x1T_ready, t + 1)
                        done(act, ssq_done, t, -1)
                        nc.scalar.activation(sq[:, u, :], bA[:, :], ACT.Square, scale=C ** -0.5).then_inc(x1_squared, 1)

                def exponent(n):
                    act.wait_ge(gate_pool, n * N_GATE_POOL + 4)
                    nc.scalar.activation(gex[:, :, :], gd[:, 0], ACT.Exp).then_inc(exp_done, 1)

                def copies(t, ks):
                    for k in ks:
                        c = BY_POOL[k]
                        act.wait_ge(gb_ready, t * CHUNKS + c + 1)
                        done(act, z_pool, t * NP, k + 1 - NP)
                        nc.scalar.copy(gbs[:, k, :], gb_bank[c % 4][:, :]).then_inc(gb_copied, 1)

                n0 = b * (TPB // 2)
                exponent(n0)
                spread_rows(t0, 0)
                with act.Fori(0, TPB // 2 - 1) as pair:
                    i = 2 * pair
                    t = t0 + i
                    copies(t, [0, 1])
                    exponent(n0 + pair + 1)
                    spread_rows(t + 1, 1)
                    copies(t, [2])
                    copies(t + 1, [0, 1])
                    spread_rows(t + 2, 0)
                    copies(t + 1, [2])
                t = t0 + TPB - 2
                copies(t, [0, 1])
                spread_rows(t + 1, 1)
                copies(t, [2])
                copies(t + 1, [0, 1, 2])

        @block.vector
        def _(dve):
            n_set = [0]

            def then(ins, wait=True):
                n_set[0] += 1
                ins.then_inc(set_dve, 1)
                if wait:
                    dve.wait_ge(set_dve, n_set[0])

            give_credit(dve, norm_done, x1_done, ssq_done, out_done, z_dve, lg_copied)
            then(dve.memset(ones16[:, :], 1.0), False)
            then(dve.memset(zeros16[:, :], 0.0), False)
            then(dve.memset(bk_rows[:, :, :], 0.0), False)
            then(dve.memset(xnT[:, :, :, :], 1.0), False)
            then(dve.memset(att[:, :], 0.0))
            dve.wait_ge(weights_in, 16 * N_LOADS)
            dve.wait_ge(const_in, 16 * 3)
            for k, width in ((0, P), (1, P), (2, C)):
                rows = P if k < 2 else C
                then(dve.tensor_reduce(w_mean[0:rows, k:k + 1], w_nat[0:rows, k, 0:width], AX_X, ALU.add))
                then(dve.tensor_scalar(w_mean[0:rows, k:k + 1], w_mean[0:rows, k:k + 1], -1.0 / C, None, ALU.mult))
                if k < 2:
                    then(dve.scalar_tensor_tensor(w_cen[:, k, :], same_half, w_mean[:, k:k + 1], w_nat[:, k, :],
                                                  ALU.mult, ALU.add))
                else:
                    then(dve.tensor_scalar(w_cen[0:C, k, :], w_nat[0:C, k, :], w_mean[0:C, k:k + 1], None, ALU.add))
            then(dve.tensor_copy(bk_part[0:1, 0, :], bk_row[0:1, 0, :]))
            then(dve.tensor_tensor(bk_row[0:1, 1, :], bk_row[0:1, 0, :], bk_part[0:1, 0, :], ALU.subtract))
            then(dve.tensor_copy(bk_part[0:1, 1, :], bk_row[0:1, 1, :]))
            then(dve.tensor_tensor(bk_row[0:1, 2, :], bk_row[0:1, 1, :], bk_part[0:1, 1, :], ALU.subtract))
            for k in range(3):
                then(dve.tensor_copy(bk_rows[32 * k:32 * k + 1, :, :],
                                     bk_row[0:1, k, :].unsqueeze(1).to_broadcast([1, NT // C, C])), False)
            then(dve.tensor_copy(eb_part[:, 0, :], eb_nat[:, :]))
            then(dve.tensor_tensor(eb_left[:, 0, :], eb_nat[:, :], eb_part[:, 0, :], ALU.subtract))
            then(dve.tensor_copy(eb_part[:, 1, :], eb_left[:, 0, :]))
            then(dve.tensor_tensor(eb_left[:, 1, :], eb_left[:, 0, :], eb_part[:, 1, :], ALU.subtract))
            then(dve.tensor_copy(eb_part[:, 2, :], eb_left[:, 1, :]))
            then(dve.tensor_scalar(eb_left[:, 0, :], eb_part[:, 0, :], part_scale[:, 0:1], None, ALU.mult))
            then(dve.scalar_tensor_tensor(eb_left[:, 1, :], eb_part[:, 1, :], part_scale[:, 1:2],
                                          eb_left[:, 0, :], ALU.mult, ALU.add))
            then(dve.scalar_tensor_tensor(eb_rows[:, :], eb_part[:, 2, :], part_scale[:, 2:3],
                                          eb_left[:, 1, :], ALU.mult, ALU.add))
            dve.wait_ge(set_pe, 1)
            then(dve.tensor_copy(wk_bd[:, :], bA[:, 0:P]), False)
            then(dve.tensor_copy(wq_bd[:, :], bB[:, 0:P]), False)
            then(dve.tensor_copy(wvT[:, :], bC[:, 0:C]), False)
            then(dve.tensor_copy(wrT[0:C, :], bD[0:C, 0:C]), False)
            then(dve.tensor_copy(ew[:, :, :].rearrange("p a c -> p (a c)"), bE[:, 0:E // 2 * C]), False)
            then(dve.tensor_copy(rw_bd[:, :], bF[:, 0:P]))
            then(dve.tensor_copy(rw_bd[:, SE:NLG], half_mean))
            assert n_set[0] == N_SET_DVE, n_set[0]

            with dve.Fori(0, BATCH) as b:
                t0 = b * TPB

                with dve.Fori(0, TPB // 2) as pair:
                    i = 2 * pair
                    for u in range(2):
                        t = t0 + i + u
                        own = t * N_STAT
                        groups = xT[:, u, :].rearrange("p (g c) -> p g c", c=C)
                        dve.wait_ge(xT_copied, t + 1)
                        dve.tensor_reduce(stat[:, 0, :], groups, AX_X, ALU.add).then_inc(stat_own, 1)
                        dve.wait_ge(stat_own, own + 1)
                        dve.scalar_tensor_tensor(stat[:, 1, :], stat[:, 0, :], 1.0 / C ** 2, stat[:, 0, :],
                                                 ALU.mult, ALU.mult).then_inc(stat_own, 1)
                        done(dve, xT_squared, t + 1)
                        dve.tensor_reduce(stat[:, 2, :], sq[:, u, :].rearrange("p (g c) -> p g c", c=C),
                                          AX_X, ALU.add).then_inc(stat_own, 1)
                        dve.wait_ge(stat_own, own + 3)
                        dve.tensor_tensor(stat[:, 3, :], stat[:, 2, :], stat[:, 1, :],
                                          ALU.subtract).then_inc(stat_own, 1)
                        dve.wait_ge(stat_own, own + 4)
                        dve.tensor_scalar(stat[:, 4, :], stat[:, 3, :], 0.0, EPS_CONV, ALU.max,
                                          ALU.add).then_inc(stat_own, 1)
                        dve.wait_ge(norm_own, t + 1)
                        done(dve, sum_done, t, -1)
                        dve.tensor_tensor(xnT[:, u, :, 0:P].rearrange("p j (s c) -> p j s c", s=S),
                                          xT[:, u, :].rearrange("p (j s c) -> p j s c", j=NJ, s=S),
                                          stat[:, 5, :].rearrange("p (j s) -> p j s", s=S).unsqueeze(3)
                                          .to_broadcast([P, NJ, S, C]), ALU.mult).then_inc(norm_done, 1)

                dve_f, pe_f = b * N_FIN_DVE, b * N_FIN_PE
                done(dve, sum_done, t0 + TPB)
                dve.tensor_copy(s_sb[:, :], bE[:, 0:P + 1]).then_inc(fin_dve, 1)
                dve.wait_ge(fin_pe, pe_f + 1)
                dve.tensor_tensor(sT_sb[:, :], bF[:, 0:P], same_half, ALU.mult).then_inc(fin_dve, 1)
                dve.wait_ge(fin_pe, pe_f + 2)
                dve.wait_ge(fin_dve, dve_f + 2)
                dve.scalar_tensor_tensor(ctx_sb[:, 1, :], bv_row[:, :], s_sb[:, P:P + 1], bG[:, 0:C],
                                         ALU.mult, ALU.add).then_inc(fin_dve, 1)
                dve.wait_ge(fin_dve, dve_f + 3)
                dve.tensor_tensor(ctx_sb[:, 0, :], ctx_sb[:, 1, :], same_head, ALU.mult).then_inc(fin_dve, 1)
                dve.wait_ge(fin_pe, pe_f + 3)
                dve.tensor_copy(ctxT_sb[:, 0, :], bF[0:C, 0:C]).then_inc(fin_dve, 1)
                dve.wait_ge(fin_dve, dve_f + 5)
                dve.tensor_tensor(ctxT_sb[:, 1, :], bF[0:C, C:P], ctxT_sb[:, 0, :], ALU.add).then_inc(fin_dve, 1)
                dve.wait_ge(fin_dve, dve_f + 6)
                dve.tensor_copy(ctxT_sb[:, 2, :], ctxT_sb[:, 1, :]).then_inc(fin_dve, 1)
                dve.wait_ge(fin_pe, pe_f + 4)
                dve.tensor_copy(att[0:C, 0:C], bG[0:C, 0:C]).then_inc(fin_dve, 1)
                dve.tensor_copy(att[C:P, C:P], bG[C:P, 0:C]).then_inc(fin_dve, 1)

                def residual(h, u):
                    t = t0 + h * 2 + u
                    dve.wait_ge(attn_ready, t + 1)
                    dve.wait_ge(x_in[u], b * (32 * TPB) + h * 32 + (16 * TPB + 32))
                    done(dve, lg_ready, t, -1)
                    done(dve, x1_kept, t, -1)
                    dve.scalar_tensor_tensor(x1[:, u, :], attn_bank[u][:, :], br_col[:, 0:1], xin[:, u, :],
                                             ALU.add, ALU.add).then_inc(x1_done, 1)

                def measure(t, i, u):
                    done(dve, x1_squared, t + 1)
                    dve.tensor_reduce(ssq[:, i + u, :], sq[:, u, :].rearrange("p (g c) -> p g c", c=C),
                                      AX_X, ALU.add).then_inc(ssq_done, 1)
                    done(dve, lg_ready, t + 1)
                    dve.tensor_copy(lg[:, bass.ds((i + u) * NJ, NJ), :],
                                    bC[:, :].rearrange("p (j n) -> p j n", j=NJ)[:, :, 0:NLG]).then_inc(lg_copied, 1)

                residual(0, 0)
                with dve.Fori(0, TPB // 2 - 1) as pair:
                    i = 2 * pair
                    for u in range(2):
                        residual(pair + u, 1 - u)
                        measure(t0 + i + u, i, u)
                residual(TPB // 2 - 1, 1)
                for u in range(2):
                    measure(t0 + TPB - 2 + u, TPB - 2, u)

                dev = b * N_DEV
                mean = lg[:, :, SE:NLG]
                done(dve, ssq_done, t0 + TPB)
                done(dve, lg_copied, t0 + TPB)
                dve.tensor_tensor(bstat[:, 0, :].rearrange("p (a s) -> p a s", s=S), mean, mean,
                                  ALU.mult).then_inc(dev_done, 1)
                dve.wait_ge(dev_done, dev + 1)
                dve.tensor_tensor(bstat[:, 1, :], ssq[:, :, :].rearrange("p t g -> p (t g)"), bstat[:, 0, :],
                                  ALU.subtract).then_inc(dev_done, 1)
                dve.wait_ge(dev_done, dev + 2)
                dve.tensor_scalar(bstat[:, 2, :], bstat[:, 1, :], 0.0, EPS_FFN, ALU.max,
                                  ALU.add).then_inc(dev_done, 1)

                def gate_steps(h):
                    n = b * (TPB // 2) + h
                    i = 2 * h
                    own, pool = n * N_GATE_DVE, n * N_GATE_POOL
                    first = first_wins.unsqueeze(1).to_broadcast([P, PG, E])
                    k = [0]

                    def step(ins):
                        k[0] += 1
                        ins.then_inc(gate_dve, 1)

                    def after():
                        dve.wait_ge(gate_dve, own + k[0])

                    def top():
                        dve.wait_ge(gate_pool, pool + 3)
                        step(dve.tensor_reduce(gstat[:, 0, :], gl[:, :, :], AX_X, ALU.max))

                    def tied(j):
                        def run():
                            if j == 0:
                                dve.wait_ge(gate_pool, pool + 4)
                            else:
                                after()
                            step(dve.scalar_tensor_tensor(gk[:, j], gd[:, j], 0.0, first, ALU.is_ge, ALU.mult))
                        return run

                    def lowest(j):
                        def run():
                            after()
                            step(dve.tensor_reduce(gstat[:, 1, :], gk[:, j], AX_X, ALU.max))
                        return run

                    def mask(j):
                        def run():
                            after()
                            step(dve.tensor_tensor(gk[:, j], gk[:, j], over_experts(gstat[:, 1, :]), ALU.is_equal))
                        return run

                    def without():
                        after()
                        step(dve.scalar_tensor_tensor(gd[:, 1], gk[:, 0], -BIG, gd[:, 0], ALU.mult, ALU.add))

                    def second():
                        after()
                        step(dve.tensor_reduce(gstat[:, 2, :], gd[:, 1], AX_X, ALU.max))

                    def below_second():
                        after()
                        step(dve.tensor_tensor(gd[:, 1], gd[:, 1], over_experts(gstat[:, 2, :]), ALU.subtract))

                    def both():
                        after()
                        step(dve.tensor_tensor(gk[:, 0], gk[:, 0], gk[:, 1], ALU.add))

                    def total():
                        dve.wait_ge(gate_pool, pool + 5)
                        step(dve.tensor_reduce(gstat[:, 3, :], gl[:, :, :], AX_X, ALU.add))

                    def inverse():
                        after()
                        step(dve.reciprocal(gstat[:, 4, :], gstat[:, 3, :]))

                    def high():
                        dve.wait_ge(gate_pool, pool + 7)
                        step(dve.tensor_copy(g2h[:, :, :, :], g2[:, :, :, :]))

                    def low(kind, k0, copies):
                        def run():
                            if kind == 0:
                                dve.wait_ge(gate_pool, pool + 8)
                                done(dve, gT_ready, b * TPB + i)
                            step(dve.tensor_scalar(
                                gT[:, :, k0 * SE:(k0 + copies) * SE].rearrange("p a (k r) -> p a k r", k=copies),
                                g2[:, :, kind, :].unsqueeze(2).to_broadcast([P, 2 * NJ, copies, SE]),
                                1.0 / LO, None, ALU.mult))
                        return run

                    steps = [top, tied(0), lowest(0), mask(0), without, second, below_second, tied(1), lowest(1),
                             mask(1), both, total, inverse, high, low(0, 1, 1), low(1, 5, 3)]
                    assert len(steps) == N_GATE_DVE
                    return steps

                def products(i, u, between):
                    t = t0 + i + u
                    dve.wait_ge(x1d_in[u], b * (32 * TPB) + i * 32 + 64)
                    for k, c in enumerate(BY_DVE):
                        dve.wait_ge(gb_ready, t * CHUNKS + c + 1)
                        done(dve, prod_done, t * CHUNKS, c - 3)
                        dve.tensor_tensor(z[:, c % 4, :], gb_bank[c % 4][:, :], x1d[:, u, c % S, :],
                                          ALU.mult).then_inc(z_dve, 1)
                        for step in between[k]:
                            step()
                    done(dve, prod_done, t * CHUNKS + CHUNKS)
                    done(dve, stored[u], b * (16 * TPB) + i * 16)
                    dve.tensor_tensor(osb[:, u, :], out_bank[u][:, :], kept[:, bass.ds((i + u) * NT, NT)],
                                      ALU.add).then_inc(out_done, 1)

                for step in gate_steps(0):
                    step()
                with dve.Fori(0, TPB // 2 - 1) as pair:
                    i = 2 * pair
                    g = gate_steps(pair + 1)
                    products(i, 0, [[], [g[0]], [g[1], g[2]], [g[3], g[4]], [g[5], g[6], g[7]]])
                    products(i, 1, [[g[8], g[9], g[10]], [g[11], g[12]], [g[13]], [g[14], g[15]], []])
                for u in range(2):
                    products(TPB - 2, u, [[]] * ND)

        @block.tensor
        def _(pe):
            def turned(dst, src, identity, step=P):
                for j in range(NJ):
                    ins = pe.transpose(dst[:, j * P:(j + 1) * P], src[:, j * step:j * step + P], identity)
                return ins

            give_credit(pe, sum_done, q_ready, lg_ready, prod_done, gT_ready)
            pe.wait_ge(const_in, 16 * 3)
            pe.wait_ge(weights_in, 16 * N_LOADS)
            pe.wait_ge(set_dve, N_SET_CEN)
            pe.transpose(bA[:, 0:P], w_cen[:, 0, :], eye)
            pe.transpose(bB[:, 0:P], w_cen[:, 1, :], eye)
            pe.transpose(bC[:, 0:C], w_cen[0:C, 2, :], eye[0:C, 0:C])
            pe.transpose(bD[0:C, 0:C], w_nat[0:C, 3, 0:C], eye[0:C, 0:C])
            pe.matmul(bE[:, 0:E // 2 * C], centre, ew_nat[:, :, :].rearrange("p a c -> p (a c)"), start=True, stop=True)
            pe.matmul(bF[:, 0:P], centre, rw_nat[:, :], start=True, stop=True).then_inc(set_pe, 1)
            pe.wait_ge(set_dve, N_SET_DVE)

            with pe.Fori(0, BATCH) as b:
                t0 = b * TPB

                def turn_x(h, u):
                    pe.wait_ge(x_in[u], b * (32 * TPB) + h * 32 + 32)
                    done(pe, xT_squared, t0 + h * 2 + u)
                    turned(bA, xin[:, u, :], eye).then_inc(xT_ready, 1)

                def turn_back(t, u):
                    done(pe, norm_done, t + 1)
                    done(pe, xn_copied, t)
                    for j in range(NJ):
                        ins = pe.transpose(bB[:, j * P:(j + 1) * P], xnT[:, u, j, 0:P], eye)
                    ins.then_inc(xn_ready, 1)

                def keys_queries(t, u):
                    done(pe, xn_copied, t + 1)
                    done(pe, k_done, t)
                    pe.matmul(bC[:, :], ones16[:, :], bk_rows[:, :, :].rearrange("p g c -> p (g c)"),
                              start=True, stop=False, skip_group_check=True)
                    for j in range(NJ):
                        ins = pe.matmul(bC[:, j * P:(j + 1) * P], xn[:, u, j * P:(j + 1) * P], wk_bd[:, :],
                                        start=False, stop=(j == NJ - 1), skip_group_check=True)
                    ins.then_inc(k_ready, 1)
                    done(pe, q_done, t)
                    pe.matmul(bD[:, :], wq_bd[:, :], xn[:, u, :], start=True, stop=True).then_inc(q_ready, 1)

                def sums(t, u, last):
                    done(pe, k_done, t + 1)
                    for j in range(NJ):
                        ins = pe.matmul(bE[:, 0:P + 1], keys[:, u, j * P:(j + 1) * P], xnT[:, u, j, :],
                                        start=False, stop=(last and j == NJ - 1), skip_group_check=True)
                    ins.then_inc(sum_done, 1)

                done(pe, out_done, t0)
                turn_x(0, 0)
                turn_x(0, 1)
                pe.matmul(bE[:, 0:P + 1], ones16[:, :], zeros16[:, :], start=True, stop=False, skip_group_check=True)
                turn_back(t0, 0)
                with pe.Fori(0, TPB // 2 - 1) as pair:
                    i = 2 * pair
                    for u in range(2):
                        t = t0 + i + u
                        keys_queries(t, u)
                        turn_x(pair + 1, u)
                        turn_back(t + 1, 1 - u)
                        sums(t, u, False)
                t = t0 + TPB - 2
                keys_queries(t, 0)
                turn_back(t + 1, 1)
                sums(t, 0, False)
                keys_queries(t + 1, 1)
                sums(t + 1, 1, True)

                dve_f = b * N_FIN_DVE
                pe.wait_ge(fin_dve, dve_f + 1)
                pe.transpose(bF[:, 0:P], s_sb[:, 0:P], eye).then_inc(fin_pe, 1)
                pe.wait_ge(fin_dve, dve_f + 2)
                pe.matmul(bG[:, 0:C], sT_sb[:, :], wvT[:, :], start=True, stop=True).then_inc(fin_pe, 1)
                pe.wait_ge(fin_dve, dve_f + 4)
                pe.transpose(bF[:, 0:P], ctx_sb[:, :, :].rearrange("p a c -> p (a c)"), eye).then_inc(fin_pe, 1)
                pe.wait_ge(fin_dve, dve_f + 7)
                pe.matmul(bG[:, 0:C], ctxT_sb[:, 1:3, :].rearrange("p a c -> p (a c)"), wrT[0:C, :],
                          start=True, stop=True).then_inc(fin_pe, 1)
                pe.wait_ge(fin_dve, dve_f + 9)

                def attend(t, i, u):
                    done(pe, x1_done, t, -1)
                    pe.matmul(attn_bank[u][:, :], att[:, :], kept[:, bass.ds(i * NT, NT)],
                              start=True, stop=True).then_inc(attn_ready, 1)

                def route(t, u):
                    done(pe, x1_done, t + 1)
                    done(pe, x1_squared, t)
                    turned(bA, x1[:, u, :], eye).then_inc(x1T_ready, 1)
                    done(pe, lg_copied, t)
                    for j in range(NJ):
                        ins = pe.matmul(bC[:, j * P:(j + 1) * P], x1[:, u, j * P:(j + 1) * P], rw_bd[:, :],
                                        start=True, stop=True)
                    ins.then_inc(lg_ready, 1)

                done(pe, q_done, t0 + TPB)
                attend(t0, 0, 0)
                with pe.Fori(0, TPB // 2 - 1) as pair:
                    i = 2 * pair
                    for u in range(2):
                        attend(t0 + i + u + 1, i + u + 1, 1 - u)
                        route(t0 + i + u, u)
                attend(t0 + TPB - 1, TPB - 1, 1)
                for u in range(2):
                    route(t0 + TPB - 2 + u, u)

                def turn_gates(h, u):
                    t = t0 + h * 2 + u
                    if u == 0:
                        pe.wait_ge(gate_dve, b * (TPB // 2 * N_GATE_DVE) + h * N_GATE_DVE + N_GATE_DVE)
                        pe.wait_ge(gate_pool, b * (TPB // 2 * N_GATE_POOL) + h * N_GATE_POOL + N_GATE_POOL)
                    done(pe, grows_done, t, -1)
                    for j in range(NJ):
                        ins = pe.transpose(gT_bank[u][:, j * C:(j + 1) * C].bitcast(F16), gT[:, u * NJ + j, :],
                                           eye16[:, :])
                    ins.then_inc(gT_ready, 1)

                def broadcast(t, c, u):
                    if c == 0:
                        done(pe, grows_done, t + 1)
                    wait_gates_read(pe, t, c - 4)
                    pe.matmul(gb_bank[c % 4][:, :], sel[:, c, :], grows[:, u, :],
                              start=True, stop=True).then_inc(gb_ready, 1)

                def experts(h, u, has_next):
                    t = t0 + h * 2 + u
                    done(pe, out_done, t, -1)
                    pe.matmul(out_bank[u][:, :], eb_rows[:, :], grows[:, u, :], start=True, stop=False,
                              skip_group_check=True)
                    for c in range(CHUNKS):
                        if c + AHEAD < CHUNKS:
                            broadcast(t, c + AHEAD, u)
                        elif has_next:
                            broadcast(t + 1, c + AHEAD - CHUNKS, 1 - u)
                        wait_product(pe, t, c)
                        s = c % S
                        pe.matmul(out_bank[u][C * s:C * s + C, :], ew[:, c // S, :], z[:, c % 4, :], start=False,
                                  stop=(c // S == E // 2 - 1), skip_group_check=True).then_inc(prod_done, 1)
                        if has_next and c == 3:
                            turn_gates(h + u, 1 - u)

                done(pe, x1_done, t0 + TPB)
                done(pe, x1_squared, t0 + TPB)
                done(pe, lg_copied, t0 + TPB)
                turn_gates(0, 0)
                for c in range(AHEAD):
                    broadcast(t0, c, 0)
                with pe.Fori(0, TPB // 2 - 1) as pair:
                    i = 2 * pair
                    for u in range(2):
                        experts(pair, u, True)
                experts(TPB // 2 - 1, 0, True)
                experts(TPB // 2 - 1, 1, False)


_INS = ['x', 'L0_conv_Wk', 'L0_conv_bk', 'L0_conv_Wq', 'L0_conv_bq', 'L0_conv_Wv', 'L0_conv_bv', 'L0_conv_Wr',
        'L0_conv_br', 'L0_ffn_router_w', 'L0_ffn_router_b', 'L0_ffn_expert_w', 'L0_ffn_expert_b']
_OUTS = [((BATCH, C, 128, 128), 'float32')]


def kernel(**inputs):
    import numpy as _np
    import concourse.bacc as _bacc
    from concourse import mybir as _mybir
    from concourse.bass_utils import run_bass_kernel_spmd as _run

    nc = _bacc.Bacc("TRN2", target_bir_lowering=False, num_devices=1)
    arrays, args = {}, []
    const = dict(zip(("const32", "const_sel", "const_eye"), constants()))
    for name, a in [(n, inputs[n]) for n in _INS] + list(const.items()):
        a = _np.ascontiguousarray(a)
        arrays[f"in_{name}_dram"] = a
        args.append(nc.dram_tensor(f"in_{name}_dram", a.shape, _mybir.dt.from_np(a.dtype), kind="ExternalInput").ap())
    for i, (shape, dtype) in enumerate(_OUTS):
        dt = _mybir.dt.from_np(_np.dtype(dtype))
        args.append(nc.dram_tensor(f"out_{i}_dram", shape, dt, kind="ExternalOutput").ap())
    metaformer_block(nc, *args)
    r = _run(nc, [arrays], core_ids=[0])
    got = tuple(r.results[0][f"out_{i}_dram"] for i in range(len(_OUTS)))
    return got[0]
```

```python
from contextlib import ExitStack

import numpy as np

import concourse.bass as bass
from concourse import mybir

ALU = mybir.AluOpType
ACT = mybir.ActivationFunctionType
AX_X = mybir.AxisListType.X
F32 = mybir.dt.float32
F16 = mybir.dt.float16
BF16 = mybir.dt.bfloat16

P = 128
BATCH, C, HW = 4, 64, 128 * 128
HEADS = 8
E = 8
S = 2
NT = 512
NJ = NT // P
TPB = HW // (S * NT)
TILES = BATCH * TPB
GR = NJ * S
SE = S * E
CHUNKS = E // 2 * S
KIND = 8
LO = 2.0 ** -11
EPS_CONV, EPS_FFN = 1e-6, 1e-5
BIG = 1e30
PG = 2 * GR
PAIRS = E // 2
AHEAD = 2
NLG = SE + S


def constants():
    eye = np.eye(P, dtype=np.float32)
    half = np.arange(P) // C
    same = (half[:, None] == half[None, :]).astype(np.float32)
    centre = eye - same / C
    ch = np.arange(P) % C
    heads = (ch[:, None] // (C // HEADS) == np.arange(C)[None, :] // (C // HEADS)).astype(np.float32)
    kind, row_s, row_e = np.arange(P) // SE, np.arange(P) // E % S, np.arange(P) % E
    parts = np.zeros((P, 3), np.float32)
    for j in range(3):
        parts[kind == 2 + j, j] = 1.0
        parts[kind == 5 + j, j] = LO
    first = np.broadcast_to(np.arange(E, 0, -1, dtype=np.float32), (P, E))
    means = np.zeros((P, S), np.float32)
    for s in range(S):
        means[half == s, s] = 1.0 / C
    f32 = np.concatenate([eye, centre, same, heads, parts, first, means], axis=1)
    sel = np.zeros((P, CHUNKS, P), np.float16)
    for p in range(E // 2):
        for s in range(S):
            for m in range(P):
                hit = (row_s == s) & (row_e == 2 * p + m // C)
                sel[hit & (kind == 0), p * S + s, m] = 1.0
                sel[hit & (kind == 1), p * S + s, m] = LO
    return np.ascontiguousarray(f32), sel.reshape(P, CHUNKS * P), np.eye(P, dtype=np.float16)


def metaformer_block(nc, x, Wk, bk, Wq, bq, Wv, bv, Wr, br, router_w, router_b, expert_w, expert_b,
                     const32, const_sel, const_eye, out):
    x_t = x.rearrange("b c h w -> b c (h w)").rearrange("b c (s i n) -> b s c i n", s=S, n=NT)
    o_t = out.rearrange("b c h w -> b c (h w)").rearrange("b c (s i n) -> b s c i n", s=S, n=NT)

    with ExitStack() as ctx:
        def sb(name, shape, dt=F32):
            return ctx.enter_context(nc.sbuf_tensor(name, shape, dt))

        def sem(name):
            return ctx.enter_context(nc.semaphore(name))

        k32 = sb("k32", [P, 3 * P + C + 3 + E + S])
        eye = k32[:, 0:P]
        centre = k32[:, P:2 * P]
        same_half = k32[:, 2 * P:3 * P]
        same_head = k32[:, 3 * P:3 * P + C]
        part_scale = k32[:, 3 * P + C:3 * P + C + 3]
        first_wins = k32[:, 3 * P + C + 3:3 * P + C + 3 + E]
        half_mean = k32[:, 3 * P + C + 3 + E:3 * P + C + 3 + E + S]
        sel = sb("sel", [P, CHUNKS, P], F16)
        eye16 = sb("eye16", [P, P], F16)
        w_nat = sb("w_nat", [P, 4, P])
        w_cen = sb("w_cen", [P, 3, P])
        w_mean = sb("w_mean", [P, 3])
        wk_bd = sb("wk_bd", [P, P])
        wq_bd = sb("wq_bd", [P, P])
        wvT = sb("wvT", [P, C])
        wrT = sb("wrT", [P, C])
        bk_row = sb("bk_row", [1, 4, C])
        bk_part = sb("bk_part", [1, 2, C], BF16)
        bk_rows = sb("bk_rows", [P, NT // C, C], BF16)
        ones16 = sb("ones16", [P, P], BF16)
        zeros16 = sb("zeros16", [P, P + 1], BF16)
        bq_col = sb("bq_col", [P, 1])
        br_col = sb("br_col", [P, 1])
        bv_row = sb("bv_row", [P, C])
        rb_row = sb("rb_row", [P, E])
        rw_nat = sb("rw_nat", [P, P])
        rw_bd = sb("rw_bd", [P, P])
        ew_nat = sb("ew_nat", [P, E // 2, C])
        ew = sb("ew", [P, E // 2, C])
        eb_nat = sb("eb_nat", [P, P])
        eb_left = sb("eb_left", [P, 2, P])
        eb_part = sb("eb_part", [P, 3, P], BF16)
        eb_rows = sb("eb_rows", [P, P], BF16)

        xin = sb("xin", [P, 2, NT])
        xT = sb("xT", [P, 2, NT])
        sq = sb("sq", [P, 2, NT])
        stat = sb("stat", [P, 7, GR])
        xnT = sb("xnT", [P, 2, NJ, P + 1])
        xn = sb("xn", [P, 2, NT])
        keys = sb("keys", [P, 2, NT])
        kept = sb("kept", [P, TPB * NT])
        s_sb = sb("s_sb", [P, P + 1])
        sT_sb = sb("sT_sb", [P, P])
        ctx_sb = sb("ctx_sb", [P, 2, C])
        ctxT_sb = sb("ctxT_sb", [C, 3, C])
        att = sb("att", [P, P])

        x1 = sb("x1", [P, 2, NT])
        lg = sb("lg", [P, TPB * NJ, NLG])
        ssq = sb("ssq", [P, TPB, GR])

        bstat = sb("bstat", [P, 5, TPB * GR])
        gstat = sb("gstat", [P, 5, PG])
        gl = sb("gl", [P, PG, E])
        gd = sb("gd", [P, 2, PG, E])
        gex = sb("gex", [P, PG, E])
        gk = sb("gk", [P, 2, PG, E])
        g2 = sb("g2", [P, 2 * NJ, 2, SE])
        gT = sb("gT", [P, 2 * NJ, P], F16)

        x1d = sb("x1d", [P, 2, S, NT])
        grows = sb("grows", [P, 2, NT], F16)
        gbs = sb("gbs", [P, PAIRS, NT])
        z = sb("z", [P, CHUNKS, NT])
        osb = sb("osb", [P, 2, NT])

        bank = [ctx.enter_context(nc.psum_tensor(f"bank{i}", [P, NT], F32)) for i in range(8)]
        bA, bB, bC, bD, bE, bF, bG, bH = bank
        attn_bank = [bB, bD]
        gb_bank = [[bC, bE], [bF, bG]]
        out_bank = [bH, bA]

        const_in = sem("const_in")
        cleared = sem("cleared")
        weights_in = sem("weights_in")
        set_dve = sem("set_dve")
        set_pe = sem("set_pe")
        x_in = [sem(f"x_in{i}") for i in range(2)]
        xT_ready = sem("xT_ready")
        xT_copied = sem("xT_copied")
        xT_squared = sem("xT_squared")
        stat_own = sem("stat_own")
        norm_own = sem("norm_own")
        dev_root = sem("dev_root")
        norm_done = sem("norm_done")
        xn_ready = sem("xn_ready")
        xn_copied = sem("xn_copied")
        k_ready = sem("k_ready")
        k_done = sem("k_done")
        q_ready = sem("q_ready")
        q_done = sem("q_done")
        sum_done = sem("sum_done")
        fin_pe = sem("fin_pe")
        fin_dve = sem("fin_dve")
        attn_ready = sem("attn_ready")
        x1_done = sem("x1_done")
        x1_kept = sem("x1_kept")
        x1T_ready = sem("x1T_ready")
        x1_squared = sem("x1_squared")
        lg_ready = sem("lg_ready")
        lg_copied = sem("lg_copied")
        ssq_done = sem("ssq_done")
        dev_done = sem("dev_done")
        gate_dve = sem("gate_dve")
        exp_done = sem("exp_done")
        high_done = sem("high_done")
        low_done = sem("low_done")
        x1d_in = [sem(f"x1d_in{i}") for i in range(2)]
        gT_ready = sem("gT_ready")
        grows_done = sem("grows_done")
        gb_ready = [sem(f"gb_ready{s}") for s in range(S)]
        gb_copied = sem("gb_copied")
        z_dve = sem("z_dve")
        z_pool = sem("z_pool")
        prod_done = sem("prod_done")
        out_done = sem("out_done")
        stored = [sem(f"stored{i}") for i in range(2)]

        credit = {norm_done: 2, sum_done: 2, q_ready: 2, lg_ready: 2, x1_kept: 2, x1_done: 2, ssq_done: 2,
                  out_done: 2, grows_done: 2, xT_squared: 1, xn_copied: 1, k_done: 1, q_done: 1, x1_squared: 1,
                  lg_copied: 1, gT_ready: 1, stored[0]: 16, stored[1]: 16,
                  z_dve: PAIRS, gb_copied: PAIRS, z_pool: PAIRS, prod_done: CHUNKS, gb_ready[0]: 2 * PAIRS}
        credit = {s.name: n for s, n in credit.items()}
        N_FIN_PE, N_FIN_DVE, N_STAT, N_DEV = 4, 9, 6, 7
        N_GATE = 20
        N_SET_CEN, N_SET_DVE = 14, 36
        N_LOADS = S * (7 + KIND - 2) + 4

        def done(eng, signal, n, more=0):
            eng.wait_ge(signal, n + (more + credit.get(signal.name, 0)))

        def give_credit(eng, *signals):
            for s in signals:
                eng.sem_inc(s, credit[s.name])

        z_done = [z_dve, z_pool]
        gates_read = [z_dve, gb_copied]

        block = ctx.enter_context(nc.Block())

        @block.sync
        def _(sp):
            count = [0]

            def load(dst, src):
                sp.dma_start(dst, src).then_inc(weights_in, 16)
                count[0] += 1

            def load_x(b, i, u):
                for s in range(S):
                    sp.dma_start(xin[C * s:C * s + C, u, :], x_t[b, s, :, i, :]).then_inc(x_in[u], 16)

            def spread(i, u):
                for s in range(S):
                    for d in range(2):
                        sp.dma_start(x1d[C * d:C * d + C, u, s, :],
                                     kept[C * s:C * s + C, bass.ds(i * NT, NT)]).then_inc(x1d_in[u], 16)

            def store(b, i, u):
                for s in range(S):
                    sp.dma_start(o_t[b, s, :, i, :], osb[C * s:C * s + C, u, :]).then_inc(stored[u], 16)

            give_credit(sp, *stored)
            sp.dma_start(k32[:, :], const32).then_inc(const_in, 16)
            sp.dma_start(sel[:, :, :].rearrange("p a b -> p (a b)"), const_sel).then_inc(const_in, 16)
            sp.dma_start(eye16[:, :], const_eye).then_inc(const_in, 16)
            sp.wait_ge(cleared, 3)
            for s in range(S):
                rows = slice(C * s, C * s + C)
                load(w_nat[rows, 0, rows], Wk)
                load(w_nat[rows, 1, rows], Wq)
                load(w_nat[0:C, 2, rows], Wv)
                load(bq_col[rows, :], bq.rearrange("(c a) -> c a", a=1))
                load(br_col[rows, :], br.rearrange("(c a) -> c a", a=1))
                load(rw_nat[rows, E * s:E * s + E], router_w)
                load(ew_nat[rows, :, :], expert_w.rearrange("(p a) d c -> a d p c", a=2)[s])
                for kind in range(2, KIND):
                    r = kind * SE + s * E
                    load(eb_nat[r:r + E, rows], expert_b)
            load(w_nat[0:C, 3, 0:C], Wr)
            load(bk_row[0:1, 0, :], bk.rearrange("(a c) -> a c", a=1))
            load(bv_row[:, :], bv.rearrange("(a c) -> a c", a=1).to_broadcast([P, C]))
            load(rb_row[:, :], router_b.rearrange("(a c) -> a c", a=1).to_broadcast([P, E]))
            assert count[0] == N_LOADS

            def batch(b, has_next):
                with sp.Fori(0, TPB // 2 - 1) as pair:
                    i = 2 * pair
                    for u in range(2):
                        done(sp, xT_ready, b * TPB + i + u + 1)
                        load_x(b, i + u + 2, u)
                for u in range(2):
                    done(sp, xT_ready, b * TPB + TPB - 1 + u)
                    load_x(b, u, u)
                with sp.Fori(0, TPB // 2 - 1) as pair:
                    i = 2 * pair
                    for u in range(2):
                        done(sp, x1_done, b * TPB + i + u + 1)
                        load_x(b, i + u + 2, u)
                done(sp, x1_kept, b * TPB + TPB)
                for u in range(2):
                    spread(u, u)
                if has_next:
                    for u in range(2):
                        load_x(b + 1, u, u)
                with sp.Fori(0, TPB // 2 - 1) as pair:
                    i = 2 * pair
                    for u in range(2):
                        t = b * TPB + i + u
                        for s in range(S):
                            done(sp, z_done[s], t * PAIRS + PAIRS)
                        spread(i + u + 2, u)
                        done(sp, out_done, t + 1)
                        store(b, i + u, u)
                for u in range(2):
                    done(sp, out_done, b * TPB + TPB - 1 + u)
                    store(b, TPB - 2 + u, u)

            for u in range(2):
                load_x(0, u, u)
            with sp.Fori(0, BATCH - 1) as b:
                batch(b, True)
            batch(BATCH - 1, False)
            for u in range(2):
                done(sp, stored[u], 16 * S * TILES // 2)

        def over_experts(a):
            return a.unsqueeze(2).to_broadcast([P, PG, E])

        def by_half(a):
            return a.rearrange("p (a s) e -> p a s e", s=S)

        def gT_kinds(k0, copies):
            return gT[:, :, k0 * SE:(k0 + copies) * SE].rearrange("p a (k r) -> p a k r", k=copies)

        def gate_copies(kind, copies):
            return g2[:, :, kind, :].unsqueeze(2).to_broadcast([P, 2 * NJ, copies, SE])

        @block.gpsimd
        def _(pool):
            for tile in (w_nat, rw_nat, eb_nat):
                pool.memset(tile[:], 0.0).then_inc(cleared, 1)
            give_credit(pool, z_pool)

            def products(b, i, u):
                t = b * TPB + i + u
                pool.wait_ge(x1d_in[u], b * (32 * TPB) + i * 32 + 64)
                for j in range(PAIRS):
                    c = j * S + 1
                    done(pool, gb_copied, t * PAIRS + j + 1)
                    done(pool, prod_done, t * CHUNKS, c + 1 - CHUNKS)
                    pool.tensor_tensor(z[:, c, :], gbs[:, j, :], x1d[:, u, 1, :], ALU.mult).then_inc(z_pool, 1)

            with pool.Fori(0, BATCH) as b:
                with pool.Fori(0, TPB // 2) as pair:
                    for u in range(2):
                        products(b, 2 * pair, u)

        @block.scalar
        def _(act):
            give_credit(act, x1_kept, grows_done, gb_copied, xT_squared, xn_copied, k_done, q_done, x1_squared)
            act.wait_ge(weights_in, 16 * N_LOADS)

            with act.Fori(0, BATCH) as b:
                def take_x(t, u):
                    act.wait_ge(xT_ready, t + 1)
                    done(act, norm_done, t, -1)
                    nc.scalar.copy(xT[:, u, :], bA[:, :]).then_inc(xT_copied, 1)
                    nc.scalar.activation(sq[:, u, :], bA[:, :], ACT.Square, scale=C ** -0.5).then_inc(xT_squared, 1)

                def root(t):
                    act.wait_ge(stat_own, t * N_STAT + N_STAT)
                    done(act, norm_done, t)
                    nc.scalar.activation(stat[:, 6, :], stat[:, 5, :], ACT.Sqrt).then_inc(norm_own, 1)

                def take_xn(t, u):
                    act.wait_ge(xn_ready, t + 1)
                    done(act, q_ready, t, -1)
                    nc.scalar.copy(xn[:, u, :], bB[:, :]).then_inc(xn_copied, 1)

                def take_kq(t, u, i):
                    act.wait_ge(k_ready, t + 1)
                    done(act, sum_done, t, -1)
                    nc.scalar.activation(keys[:, u, :], bC[:, :], ACT.Relu).then_inc(k_done, 1)
                    done(act, q_ready, t + 1)
                    nc.scalar.activation(kept[:, bass.ds(i * NT, NT)], bD[:, :], ACT.Relu,
                                         bias=bq_col[:, 0:1]).then_inc(q_done, 1)

                t0 = b * TPB
                take_x(t0, 0)
                root(t0)
                take_x(t0 + 1, 1)
                take_xn(t0, 0)
                with act.Fori(0, TPB // 2 - 1) as pair:
                    i = 2 * pair
                    for u in range(2):
                        root(t0 + i + u + 1)
                        take_kq(t0 + i + u, u, i + u)
                        take_x(t0 + i + u + 2, u)
                        take_xn(t0 + i + u + 1, 1 - u)
                root(t0 + TPB - 1)
                take_kq(t0 + TPB - 2, 0, TPB - 2)
                take_xn(t0 + TPB - 1, 1)
                take_kq(t0 + TPB - 1, 1, TPB - 1)

                with act.Fori(0, TPB // 2) as pair:
                    i = 2 * pair
                    for u in range(2):
                        t = t0 + i + u
                        done(act, x1_done, t + 1)
                        done(act, attn_ready, t + 1)
                        nc.scalar.copy(kept[:, bass.ds((i + u) * NT, NT)], x1[:, u, :]).then_inc(x1_kept, 1)
                        act.wait_ge(x1T_ready, t + 1)
                        done(act, ssq_done, t, -1)
                        nc.scalar.activation(sq[:, u, :], bA[:, :], ACT.Square, scale=C ** -0.5).then_inc(x1_squared, 1)
                act.wait_ge(dev_done, b * N_DEV + 4)
                nc.scalar.activation(bstat[:, 4, :], bstat[:, 3, :], ACT.Sqrt).then_inc(dev_root, 1)

                n0 = b * (TPB // 2)

                def exponent(n):
                    act.wait_ge(gate_dve, n * N_GATE + 4)
                    nc.scalar.activation(gex[:, :, :], gd[:, 0], ACT.Exp).then_inc(exp_done, 1)

                def high(n):
                    act.wait_ge(gate_dve, n * N_GATE + 19)
                    done(act, gT_ready, n)
                    for kind, k0, copies in ((0, 0, 1), (1, 2, 3)):
                        nc.scalar.copy(gT_kinds(k0, copies), gate_copies(kind, copies)).then_inc(high_done, 1)

                def low(n):
                    act.wait_ge(gate_dve, n * N_GATE + 20)
                    for kind, k0, copies in ((0, 1, 1), (1, 5, 3)):
                        nc.scalar.activation(gT_kinds(k0, copies), gate_copies(kind, copies), ACT.Copy,
                                             scale=1.0 / LO).then_inc(low_done, 1)

                def gate_rows(n, t, u):
                    done(act, gT_ready, n + 1)
                    done(act, gb_ready[0], t * PAIRS, -PAIRS)
                    nc.scalar.copy(grows[:, u, :], bB[:, u * (NT // 2):(u + 1) * (NT // 2)].bitcast(F16)
                                   ).then_inc(grows_done, 1)

                def copy_gates(t, *js):
                    for j in js:
                        act.wait_ge(gb_ready[1], t * PAIRS + j + 1)
                        done(act, z_pool, t * PAIRS, j + 1 - PAIRS)
                        nc.scalar.copy(gbs[:, j, :], gb_bank[1][j % 2][:, :]).then_inc(gb_copied, 1)

                exponent(n0)
                high(n0)
                low(n0)
                gate_rows(n0, t0, 0)
                gate_rows(n0, t0 + 1, 1)
                copy_gates(t0, 0, 1)
                exponent(n0 + 1)

                def pair_of_tiles(h, has_next, has_second_next):
                    n, t = n0 + h, t0 + h * 2
                    copy_gates(t, 2, 3)
                    copy_gates(t + 1, 0)
                    if has_next:
                        high(n + 1)
                    copy_gates(t + 1, 1)
                    if has_next:
                        low(n + 1)
                    copy_gates(t + 1, 2, 3)
                    if has_next:
                        gate_rows(n + 1, t + 2, 0)
                    if has_second_next:
                        exponent(n + 2)
                    if has_next:
                        copy_gates(t + 2, 0, 1)
                        gate_rows(n + 1, t + 3, 1)

                with act.Fori(0, TPB // 2 - 2) as pair:
                    pair_of_tiles(pair, True, True)
                pair_of_tiles(TPB // 2 - 2, True, False)
                pair_of_tiles(TPB // 2 - 1, False, False)

        @block.vector
        def _(dve):
            n_set = [0]

            def then(ins, wait=True):
                n_set[0] += 1
                ins.then_inc(set_dve, 1)
                if wait:
                    dve.wait_ge(set_dve, n_set[0])

            give_credit(dve, norm_done, x1_done, ssq_done, out_done, z_dve, lg_copied)
            then(dve.memset(ones16[:, :], 1.0), False)
            then(dve.memset(zeros16[:, :], 0.0), False)
            then(dve.memset(bk_rows[:, :, :], 0.0), False)
            then(dve.memset(xnT[:, :, :, :], 1.0), False)
            then(dve.memset(att[:, :], 0.0))
            dve.wait_ge(weights_in, 16 * N_LOADS)
            dve.wait_ge(const_in, 16 * 3)
            for k, width in ((0, P), (1, P), (2, C)):
                rows = P if k < 2 else C
                then(dve.tensor_reduce(w_mean[0:rows, k:k + 1], w_nat[0:rows, k, 0:width], AX_X, ALU.add))
                then(dve.tensor_scalar(w_mean[0:rows, k:k + 1], w_mean[0:rows, k:k + 1], -1.0 / C, None, ALU.mult))
                if k < 2:
                    then(dve.scalar_tensor_tensor(w_cen[:, k, :], same_half, w_mean[:, k:k + 1], w_nat[:, k, :],
                                                  ALU.mult, ALU.add))
                else:
                    then(dve.tensor_scalar(w_cen[0:C, k, :], w_nat[0:C, k, :], w_mean[0:C, k:k + 1], None, ALU.add))
            then(dve.tensor_copy(bk_part[0:1, 0, :], bk_row[0:1, 0, :]))
            then(dve.tensor_tensor(bk_row[0:1, 1, :], bk_row[0:1, 0, :], bk_part[0:1, 0, :], ALU.subtract))
            then(dve.tensor_copy(bk_part[0:1, 1, :], bk_row[0:1, 1, :]))
            then(dve.tensor_tensor(bk_row[0:1, 2, :], bk_row[0:1, 1, :], bk_part[0:1, 1, :], ALU.subtract))
            for k in range(3):
                then(dve.tensor_copy(bk_rows[32 * k:32 * k + 1, :, :],
                                     bk_row[0:1, k, :].unsqueeze(1).to_broadcast([1, NT // C, C])), False)
            then(dve.tensor_copy(eb_part[:, 0, :], eb_nat[:, :]))
            then(dve.tensor_tensor(eb_left[:, 0, :], eb_nat[:, :], eb_part[:, 0, :], ALU.subtract))
            then(dve.tensor_copy(eb_part[:, 1, :], eb_left[:, 0, :]))
            then(dve.tensor_tensor(eb_left[:, 1, :], eb_left[:, 0, :], eb_part[:, 1, :], ALU.subtract))
            then(dve.tensor_copy(eb_part[:, 2, :], eb_left[:, 1, :]))
            then(dve.tensor_scalar(eb_left[:, 0, :], eb_part[:, 0, :], part_scale[:, 0:1], None, ALU.mult))
            then(dve.scalar_tensor_tensor(eb_left[:, 1, :], eb_part[:, 1, :], part_scale[:, 1:2],
                                          eb_left[:, 0, :], ALU.mult, ALU.add))
            then(dve.scalar_tensor_tensor(eb_rows[:, :], eb_part[:, 2, :], part_scale[:, 2:3],
                                          eb_left[:, 1, :], ALU.mult, ALU.add))
            dve.wait_ge(set_pe, 1)
            then(dve.tensor_copy(wk_bd[:, :], bA[:, 0:P]), False)
            then(dve.tensor_copy(wq_bd[:, :], bB[:, 0:P]), False)
            then(dve.tensor_copy(wvT[:, :], bC[:, 0:C]), False)
            then(dve.tensor_copy(wrT[0:C, :], bD[0:C, 0:C]), False)
            then(dve.tensor_copy(ew[:, :, :].rearrange("p a c -> p (a c)"), bE[:, 0:E // 2 * C]), False)
            then(dve.tensor_copy(rw_bd[:, :], bF[:, 0:P]))
            then(dve.tensor_copy(rw_bd[:, SE:NLG], half_mean))
            assert n_set[0] == N_SET_DVE, n_set[0]

            with dve.Fori(0, BATCH) as b:
                t0 = b * TPB

                with dve.Fori(0, TPB // 2) as pair:
                    i = 2 * pair
                    for u in range(2):
                        t = t0 + i + u
                        own = t * N_STAT
                        groups = xT[:, u, :].rearrange("p (g c) -> p g c", c=C)
                        dve.wait_ge(xT_copied, t + 1)
                        dve.tensor_reduce(stat[:, 0, :], groups, AX_X, ALU.add).then_inc(stat_own, 1)
                        dve.wait_ge(stat_own, own + 1)
                        dve.scalar_tensor_tensor(stat[:, 1, :], stat[:, 0, :], 1.0 / C ** 2, stat[:, 0, :],
                                                 ALU.mult, ALU.mult).then_inc(stat_own, 1)
                        done(dve, xT_squared, t + 1)
                        dve.tensor_reduce(stat[:, 2, :], sq[:, u, :].rearrange("p (g c) -> p g c", c=C),
                                          AX_X, ALU.add).then_inc(stat_own, 1)
                        dve.wait_ge(stat_own, own + 3)
                        dve.tensor_tensor(stat[:, 3, :], stat[:, 2, :], stat[:, 1, :],
                                          ALU.subtract).then_inc(stat_own, 1)
                        dve.wait_ge(stat_own, own + 4)
                        dve.tensor_scalar(stat[:, 4, :], stat[:, 3, :], 0.0, EPS_CONV, ALU.max,
                                          ALU.add).then_inc(stat_own, 1)
                        dve.wait_ge(stat_own, own + 5)
                        dve.reciprocal(stat[:, 5, :], stat[:, 4, :]).then_inc(stat_own, 1)
                        dve.wait_ge(norm_own, t + 1)
                        done(dve, sum_done, t, -1)
                        dve.tensor_tensor(xnT[:, u, :, 0:P].rearrange("p j (s c) -> p j s c", s=S),
                                          xT[:, u, :].rearrange("p (j s c) -> p j s c", j=NJ, s=S),
                                          stat[:, 6, :].rearrange("p (j s) -> p j s", s=S).unsqueeze(3)
                                          .to_broadcast([P, NJ, S, C]), ALU.mult).then_inc(norm_done, 1)

                dve_f, pe_f = b * N_FIN_DVE, b * N_FIN_PE
                done(dve, sum_done, t0 + TPB)
                dve.tensor_copy(s_sb[:, :], bE[:, 0:P + 1]).then_inc(fin_dve, 1)
                dve.wait_ge(fin_pe, pe_f + 1)
                dve.tensor_tensor(sT_sb[:, :], bF[:, 0:P], same_half, ALU.mult).then_inc(fin_dve, 1)
                dve.wait_ge(fin_pe, pe_f + 2)
                dve.wait_ge(fin_dve, dve_f + 2)
                dve.scalar_tensor_tensor(ctx_sb[:, 1, :], bv_row[:, :], s_sb[:, P:P + 1], bG[:, 0:C],
                                         ALU.mult, ALU.add).then_inc(fin_dve, 1)
                dve.wait_ge(fin_dve, dve_f + 3)
                dve.tensor_tensor(ctx_sb[:, 0, :], ctx_sb[:, 1, :], same_head, ALU.mult).then_inc(fin_dve, 1)
                dve.wait_ge(fin_pe, pe_f + 3)
                dve.tensor_copy(ctxT_sb[:, 0, :], bF[0:C, 0:C]).then_inc(fin_dve, 1)
                dve.wait_ge(fin_dve, dve_f + 5)
                dve.tensor_tensor(ctxT_sb[:, 1, :], bF[0:C, C:P], ctxT_sb[:, 0, :], ALU.add).then_inc(fin_dve, 1)
                dve.wait_ge(fin_dve, dve_f + 6)
                dve.tensor_copy(ctxT_sb[:, 2, :], ctxT_sb[:, 1, :]).then_inc(fin_dve, 1)
                dve.wait_ge(fin_pe, pe_f + 4)
                dve.tensor_copy(att[0:C, 0:C], bG[0:C, 0:C]).then_inc(fin_dve, 1)
                dve.tensor_copy(att[C:P, C:P], bG[C:P, 0:C]).then_inc(fin_dve, 1)

                def residual(h, u):
                    t = t0 + h * 2 + u
                    dve.wait_ge(attn_ready, t + 1)
                    dve.wait_ge(x_in[u], b * (32 * TPB) + h * 32 + (16 * TPB + 32))
                    done(dve, lg_ready, t, -1)
                    done(dve, x1_kept, t, -1)
                    dve.scalar_tensor_tensor(x1[:, u, :], attn_bank[u][:, :], br_col[:, 0:1], xin[:, u, :],
                                             ALU.add, ALU.add).then_inc(x1_done, 1)

                def measure(t, i, u):
                    done(dve, x1_squared, t + 1)
                    dve.tensor_reduce(ssq[:, i + u, :], sq[:, u, :].rearrange("p (g c) -> p g c", c=C),
                                      AX_X, ALU.add).then_inc(ssq_done, 1)
                    done(dve, lg_ready, t + 1)
                    dve.tensor_copy(lg[:, bass.ds((i + u) * NJ, NJ), :],
                                    bC[:, :].rearrange("p (j n) -> p j n", j=NJ)[:, :, 0:NLG]).then_inc(lg_copied, 1)

                residual(0, 0)
                with dve.Fori(0, TPB // 2 - 1) as pair:
                    i = 2 * pair
                    for u in range(2):
                        residual(pair + u, 1 - u)
                        measure(t0 + i + u, i, u)
                residual(TPB // 2 - 1, 1)
                for u in range(2):
                    measure(t0 + TPB - 2 + u, TPB - 2, u)

                dev = b * N_DEV
                mean = lg[:, :, SE:NLG]
                done(dve, ssq_done, t0 + TPB)
                done(dve, lg_copied, t0 + TPB)
                dve.tensor_tensor(bstat[:, 0, :].rearrange("p (a s) -> p a s", s=S), mean, mean,
                                  ALU.mult).then_inc(dev_done, 1)
                dve.wait_ge(dev_done, dev + 1)
                dve.tensor_tensor(bstat[:, 1, :], ssq[:, :, :].rearrange("p t g -> p (t g)"), bstat[:, 0, :],
                                  ALU.subtract).then_inc(dev_done, 1)
                dve.wait_ge(dev_done, dev + 2)
                dve.tensor_scalar(bstat[:, 2, :], bstat[:, 1, :], 0.0, EPS_FFN, ALU.max,
                                  ALU.add).then_inc(dev_done, 1)
                dve.wait_ge(dev_done, dev + 3)
                dve.reciprocal(bstat[:, 3, :], bstat[:, 2, :]).then_inc(dev_done, 1)

                dve.wait_ge(dev_root, b + 1)
                dve.scalar_tensor_tensor(bstat[:, 0, :], bstat[:, 4, :], -0.5, bstat[:, 4, :],
                                         ALU.mult, ALU.mult).then_inc(dev_done, 1)
                dve.wait_ge(dev_done, dev + 5)
                dve.tensor_tensor(bstat[:, 1, :], bstat[:, 0, :], bstat[:, 2, :], ALU.mult).then_inc(dev_done, 1)
                dve.wait_ge(dev_done, dev + 6)
                dve.scalar_tensor_tensor(bstat[:, 4, :], bstat[:, 1, :], 1.5, bstat[:, 4, :],
                                         ALU.add, ALU.mult).then_inc(dev_done, 1)
                dve.wait_ge(dev_done, dev + 7)

                def gate_steps(h, taken=0):
                    n = b * (TPB // 2) + h
                    own = n * N_GATE
                    first = first_wins.unsqueeze(1).to_broadcast([P, PG, E])
                    kinds = g2[:, :, :, :].rearrange("p a k (s e) -> p a k s e", s=S)
                    over_dev = by_half(over_experts(bstat[:, 4, bass.ds(h * PG, PG)]))
                    k = [taken]

                    def step(fn):
                        def run():
                            if k[0]:
                                dve.wait_ge(gate_dve, own + k[0])
                            k[0] += 1
                            fn().then_inc(gate_dve, 1)
                        return run

                    def choose():
                        dve.wait_ge(exp_done, n + 1)
                        return dve.tensor_tensor(gl[:, :, :], gex[:, :, :], gk[:, 0], ALU.mult)

                    def left():
                        dve.wait_ge(high_done, n * 2 + 2)
                        return dve.tensor_tensor(g2[:, :, :, :], g2[:, :, :, :],
                                                 gT[:, :, :].rearrange("p a (k r) -> p a k r", r=SE)[:, :, 0:3:2, :],
                                                 ALU.subtract)

                    def scale():
                        if not (isinstance(h, int) and h == 0):
                            dve.wait_ge(low_done, n * 2)
                        return dve.tensor_tensor(by_half(gl[:, :, :]),
                                                 lg[:, bass.ds(h * (2 * NJ), 2 * NJ), 0:SE]
                                                 .rearrange("p a (s e) -> p a s e", s=S), over_dev, ALU.mult)

                    def tied(j):
                        return lambda: dve.scalar_tensor_tensor(gk[:, j], gd[:, j], 0.0, first, ALU.is_ge, ALU.mult)

                    def lowest(j):
                        return lambda: dve.tensor_reduce(gstat[:, 1, :], gk[:, j], AX_X, ALU.max)

                    def mask(j):
                        return lambda: dve.tensor_tensor(gk[:, j], gk[:, j], over_experts(gstat[:, 1, :]),
                                                         ALU.is_equal)

                    steps = [
                        scale,
                        lambda: dve.tensor_tensor(gl[:, :, :], gl[:, :, :],
                                                  rb_row[:, :].unsqueeze(1).to_broadcast([P, PG, E]), ALU.add),
                        lambda: dve.tensor_reduce(gstat[:, 0, :], gl[:, :, :], AX_X, ALU.max),
                        lambda: dve.tensor_tensor(gd[:, 0], gl[:, :, :], over_experts(gstat[:, 0, :]), ALU.subtract),
                        tied(0), lowest(0), mask(0),
                        lambda: dve.scalar_tensor_tensor(gd[:, 1], gk[:, 0], -BIG, gd[:, 0], ALU.mult, ALU.add),
                        lambda: dve.tensor_reduce(gstat[:, 2, :], gd[:, 1], AX_X, ALU.max),
                        lambda: dve.tensor_tensor(gd[:, 1], gd[:, 1], over_experts(gstat[:, 2, :]), ALU.subtract),
                        tied(1), lowest(1), mask(1),
                        lambda: dve.tensor_tensor(gk[:, 0], gk[:, 0], gk[:, 1], ALU.add),
                        choose,
                        lambda: dve.tensor_reduce(gstat[:, 3, :], gl[:, :, :], AX_X, ALU.add),
                        lambda: dve.reciprocal(gstat[:, 4, :], gstat[:, 3, :]),
                        lambda: dve.tensor_tensor(kinds[:, :, 1], by_half(gl[:, :, :]),
                                                  by_half(over_experts(gstat[:, 4, :])), ALU.mult),
                        lambda: dve.tensor_tensor(kinds[:, :, 0], kinds[:, :, 1], over_dev, ALU.mult),
                        left]
                    assert len(steps) == N_GATE
                    return [step(fn) for fn in steps]

                def product(h, u, j, *between):
                    t = t0 + h * 2 + u
                    if j == 0:
                        dve.wait_ge(x1d_in[u], b * (32 * TPB) + h * 64 + 64)
                    c = j * S
                    done(dve, gb_ready[0], t * PAIRS + j + 1)
                    done(dve, prod_done, t * CHUNKS, c + 1 - CHUNKS)
                    dve.tensor_tensor(z[:, c, :], gb_bank[0][j % 2][:, :], x1d[:, u, 0, :],
                                      ALU.mult).then_inc(z_dve, 1)
                    for step in between:
                        step()

                def result(h, u, *between):
                    t = t0 + h * 2 + u
                    done(dve, prod_done, t * CHUNKS + CHUNKS)
                    done(dve, stored[u], b * (16 * TPB) + h * 32)
                    dve.tensor_tensor(osb[:, u, :], out_bank[u][:, :], kept[:, bass.ds(h * (2 * NT) + u * NT, NT)],
                                      ALU.add).then_inc(out_done, 1)
                    for step in between:
                        step()

                def pair_of_tiles(h, now, ahead, has_next):
                    g, f = now or [lambda: None] * N_GATE, ahead or [lambda: None] * N_GATE
                    product(h, 0, 1, *g[10:13])
                    product(h, 0, 2, *g[13:16])
                    product(h, 0, 3, *g[16:19])
                    product(h, 1, 0, *g[19:20])
                    result(h, 0)
                    product(h, 1, 1, *f[0:2])
                    product(h, 1, 2, *f[2:4])
                    product(h, 1, 3, *f[4:6])
                    if has_next:
                        product(h + 1, 0, 0, *f[6:8])
                    result(h, 1, *f[8:10])

                for step in gate_steps(0):
                    step()
                product(0, 0, 0)
                for step in gate_steps(1)[0:10]:
                    step()
                with dve.Fori(0, TPB // 2 - 2) as pair:
                    now = gate_steps(pair + 1, 10)
                    pair_of_tiles(pair, now, gate_steps(pair + 2), True)
                pair_of_tiles(TPB // 2 - 2, gate_steps(TPB // 2 - 1, 10), None, True)
                pair_of_tiles(TPB // 2 - 1, None, None, False)

        @block.tensor
        def _(pe):
            def turned(dst, src, identity, step=P):
                for j in range(NJ):
                    ins = pe.transpose(dst[:, j * P:(j + 1) * P], src[:, j * step:j * step + P], identity)
                return ins

            give_credit(pe, sum_done, q_ready, lg_ready, prod_done, gT_ready, gb_ready[0])
            pe.wait_ge(const_in, 16 * 3)
            pe.wait_ge(weights_in, 16 * N_LOADS)
            pe.wait_ge(set_dve, N_SET_CEN)
            pe.transpose(bA[:, 0:P], w_cen[:, 0, :], eye)
            pe.transpose(bB[:, 0:P], w_cen[:, 1, :], eye)
            pe.transpose(bC[:, 0:C], w_cen[0:C, 2, :], eye[0:C, 0:C])
            pe.transpose(bD[0:C, 0:C], w_nat[0:C, 3, 0:C], eye[0:C, 0:C])
            pe.matmul(bE[:, 0:E // 2 * C], centre, ew_nat[:, :, :].rearrange("p a c -> p (a c)"), start=True, stop=True)
            pe.matmul(bF[:, 0:P], centre, rw_nat[:, :], start=True, stop=True).then_inc(set_pe, 1)
            pe.wait_ge(set_dve, N_SET_DVE)

            with pe.Fori(0, BATCH) as b:
                t0 = b * TPB

                def turn_x(h, u):
                    pe.wait_ge(x_in[u], b * (32 * TPB) + h * 32 + 32)
                    done(pe, xT_squared, t0 + h * 2 + u)
                    turned(bA, xin[:, u, :], eye).then_inc(xT_ready, 1)

                def turn_back(t, u):
                    done(pe, norm_done, t + 1)
                    done(pe, xn_copied, t)
                    for j in range(NJ):
                        ins = pe.transpose(bB[:, j * P:(j + 1) * P], xnT[:, u, j, 0:P], eye)
                    ins.then_inc(xn_ready, 1)

                def keys_queries(t, u):
                    done(pe, xn_copied, t + 1)
                    done(pe, k_done, t)
                    pe.matmul(bC[:, :], ones16[:, :], bk_rows[:, :, :].rearrange("p g c -> p (g c)"),
                              start=True, stop=False, skip_group_check=True)
                    for j in range(NJ):
                        ins = pe.matmul(bC[:, j * P:(j + 1) * P], xn[:, u, j * P:(j + 1) * P], wk_bd[:, :],
                                        start=False, stop=(j == NJ - 1), skip_group_check=True)
                    ins.then_inc(k_ready, 1)
                    done(pe, q_done, t)
                    pe.matmul(bD[:, :], wq_bd[:, :], xn[:, u, :], start=True, stop=True).then_inc(q_ready, 1)

                def sums(t, u, last):
                    done(pe, k_done, t + 1)
                    for j in range(NJ):
                        ins = pe.matmul(bE[:, 0:P + 1], keys[:, u, j * P:(j + 1) * P], xnT[:, u, j, :],
                                        start=False, stop=(last and j == NJ - 1), skip_group_check=True)
                    ins.then_inc(sum_done, 1)

                done(pe, out_done, t0)
                turn_x(0, 0)
                turn_x(0, 1)
                pe.matmul(bE[:, 0:P + 1], ones16[:, :], zeros16[:, :], start=True, stop=False, skip_group_check=True)
                turn_back(t0, 0)
                with pe.Fori(0, TPB // 2 - 1) as pair:
                    i = 2 * pair
                    for u in range(2):
                        t = t0 + i + u
                        keys_queries(t, u)
                        turn_x(pair + 1, u)
                        turn_back(t + 1, 1 - u)
                        sums(t, u, False)
                t = t0 + TPB - 2
                keys_queries(t, 0)
                turn_back(t + 1, 1)
                sums(t, 0, False)
                keys_queries(t + 1, 1)
                sums(t + 1, 1, True)

                dve_f = b * N_FIN_DVE
                pe.wait_ge(fin_dve, dve_f + 1)
                pe.transpose(bF[:, 0:P], s_sb[:, 0:P], eye).then_inc(fin_pe, 1)
                pe.wait_ge(fin_dve, dve_f + 2)
                pe.matmul(bG[:, 0:C], sT_sb[:, :], wvT[:, :], start=True, stop=True).then_inc(fin_pe, 1)
                pe.wait_ge(fin_dve, dve_f + 4)
                pe.transpose(bF[:, 0:P], ctx_sb[:, :, :].rearrange("p a c -> p (a c)"), eye).then_inc(fin_pe, 1)
                pe.wait_ge(fin_dve, dve_f + 7)
                pe.matmul(bG[:, 0:C], ctxT_sb[:, 1:3, :].rearrange("p a c -> p (a c)"), wrT[0:C, :],
                          start=True, stop=True).then_inc(fin_pe, 1)
                pe.wait_ge(fin_dve, dve_f + 9)

                def attend(t, i, u):
                    done(pe, x1_done, t, -1)
                    pe.matmul(attn_bank[u][:, :], att[:, :], kept[:, bass.ds(i * NT, NT)],
                              start=True, stop=True).then_inc(attn_ready, 1)

                def route(t, u):
                    done(pe, x1_done, t + 1)
                    done(pe, x1_squared, t)
                    turned(bA, x1[:, u, :], eye).then_inc(x1T_ready, 1)
                    done(pe, lg_copied, t)
                    for j in range(NJ):
                        ins = pe.matmul(bC[:, j * P:(j + 1) * P], x1[:, u, j * P:(j + 1) * P], rw_bd[:, :],
                                        start=True, stop=True)
                    ins.then_inc(lg_ready, 1)

                done(pe, q_done, t0 + TPB)
                attend(t0, 0, 0)
                with pe.Fori(0, TPB // 2 - 1) as pair:
                    i = 2 * pair
                    for u in range(2):
                        attend(t0 + i + u + 1, i + u + 1, 1 - u)
                        route(t0 + i + u, u)
                attend(t0 + TPB - 1, TPB - 1, 1)
                for u in range(2):
                    route(t0 + TPB - 2 + u, u)

                def turn_gates(h):
                    pe.wait_ge(low_done, b * TPB + h * 2 + 2)
                    done(pe, grows_done, t0 + h * 2)
                    for j in range(2 * NJ):
                        ins = pe.transpose(bB[:, j * C:(j + 1) * C].bitcast(F16), gT[:, j, :], eye16[:, :])
                    ins.then_inc(gT_ready, 1)

                def broadcast(t, u, j, s):
                    if s == 1 and j == 0:
                        done(pe, grows_done, t + 1)
                    done(pe, gates_read[s], t * PAIRS, j - 1)
                    pe.matmul(gb_bank[s][j % 2][:, :], sel[:, j * S + s, :], grows[:, u, :],
                              start=True, stop=True).then_inc(gb_ready[s], 1)

                def experts(h, u, has_next, turn):
                    t = t0 + h * 2 + u
                    done(pe, out_done, t, -1)
                    pe.matmul(out_bank[u][:, :], eb_rows[:, :], grows[:, u, :], start=True, stop=False,
                              skip_group_check=True)
                    for j in range(PAIRS):
                        if turn and j == 1:
                            turn_gates(h + 1)
                        for s in (1, 0):
                            if j + AHEAD < PAIRS:
                                broadcast(t, u, j + AHEAD, s)
                            elif has_next:
                                broadcast(t + 1, 1 - u, j + AHEAD - PAIRS, s)
                        for s in range(S):
                            done(pe, z_done[s], t * PAIRS + j + 1)
                            pe.matmul(out_bank[u][C * s:C * s + C, :], ew[:, j, :], z[:, j * S + s, :], start=False,
                                      stop=(j == PAIRS - 1), skip_group_check=True).then_inc(prod_done, 1)

                done(pe, x1_done, t0 + TPB)
                done(pe, x1_squared, t0 + TPB)
                done(pe, lg_copied, t0 + TPB)
                turn_gates(0)
                for j in range(AHEAD):
                    for s in (1, 0):
                        broadcast(t0, 0, j, s)
                with pe.Fori(0, TPB // 2 - 1) as pair:
                    experts(pair, 0, True, False)
                    experts(pair, 1, True, True)
                experts(TPB // 2 - 1, 0, True, False)
                experts(TPB // 2 - 1, 1, False, False)


_INS = ['x', 'L0_conv_Wk', 'L0_conv_bk', 'L0_conv_Wq', 'L0_conv_bq', 'L0_conv_Wv', 'L0_conv_bv', 'L0_conv_Wr',
        'L0_conv_br', 'L0_ffn_router_w', 'L0_ffn_router_b', 'L0_ffn_expert_w', 'L0_ffn_expert_b']
_OUTS = [((BATCH, C, 128, 128), 'float32')]


def kernel(**inputs):
    import numpy as _np
    import concourse.bacc as _bacc
    from concourse import mybir as _mybir
    from concourse.bass_utils import run_bass_kernel_spmd as _run

    nc = _bacc.Bacc("TRN2", target_bir_lowering=False, num_devices=1)
    arrays, args = {}, []
    const = dict(zip(("const32", "const_sel", "const_eye"), constants()))
    for name, a in [(n, inputs[n]) for n in _INS] + list(const.items()):
        a = _np.ascontiguousarray(a)
        arrays[f"in_{name}_dram"] = a
        args.append(nc.dram_tensor(f"in_{name}_dram", a.shape, _mybir.dt.from_np(a.dtype), kind="ExternalInput").ap())
    for i, (shape, dtype) in enumerate(_OUTS):
        dt = _mybir.dt.from_np(_np.dtype(dtype))
        args.append(nc.dram_tensor(f"out_{i}_dram", shape, dt, kind="ExternalOutput").ap())
    metaformer_block(nc, *args)
    r = _run(nc, [arrays], core_ids=[0])
    got = tuple(r.results[0][f"out_{i}_dram"] for i in range(len(_OUTS)))
    return got[0]
```

```python
from contextlib import ExitStack

import numpy as np

import concourse.bass as bass
from concourse import mybir

ALU = mybir.AluOpType
ACT = mybir.ActivationFunctionType
AX_X = mybir.AxisListType.X
F32 = mybir.dt.float32
F16 = mybir.dt.float16
BF16 = mybir.dt.bfloat16

P = 128
BATCH, C, HW = 4, 64, 128 * 128
HEADS = 8
E = 8
S = 2
NT = 512
NJ = NT // P
TPB = HW // (S * NT)
TILES = BATCH * TPB
GR = NJ * S
SE = S * E
CHUNKS = E // 2 * S
KIND = 8
LO = 2.0 ** -11
EPS_CONV, EPS_FFN = 1e-6, 1e-5
BIG = 1e30
QUAD = 4
QUADS = TPB // QUAD
QJ, QG = QUAD * NJ, QUAD * GR
PAIRS = E // 2
AHEAD_STEPS = 6
AHEAD = 2
NLG = SE + S


def constants():
    eye = np.eye(P, dtype=np.float32)
    half = np.arange(P) // C
    same = (half[:, None] == half[None, :]).astype(np.float32)
    centre = eye - same / C
    ch = np.arange(P) % C
    heads = (ch[:, None] // (C // HEADS) == ch[None, :] // (C // HEADS)).astype(np.float32)
    both = (ch[:, None] == ch[None, :]).astype(np.float32)
    kind, row_s, row_e = np.arange(P) // SE, np.arange(P) // E % S, np.arange(P) % E
    parts = np.zeros((P, 3), np.float32)
    for j in range(3):
        parts[kind == 2 + j, j] = 1.0
        parts[kind == 5 + j, j] = LO
    first = np.broadcast_to(np.arange(E, 0, -1, dtype=np.float32), (P, E))
    means = np.zeros((P, S), np.float32)
    for s in range(S):
        means[half == s, s] = 1.0 / C
    bias_rows = np.zeros((P, P), np.float32)
    for k in range(2, KIND):
        bias_rows[:SE, k * SE:(k + 1) * SE] = np.eye(SE)
    f32 = np.concatenate([eye, centre, same, heads, parts, first, means, bias_rows, both], axis=1)
    sel = np.zeros((P, CHUNKS, P), np.float16)
    for p in range(E // 2):
        for s in range(S):
            for m in range(P):
                hit = (row_s == s) & (row_e == 2 * p + m // C)
                sel[hit & (kind == 0), p * S + s, m] = 1.0
                sel[hit & (kind == 1), p * S + s, m] = LO
    return np.ascontiguousarray(f32), sel.reshape(P, CHUNKS * P), np.eye(P, dtype=np.float16)


def metaformer_block(nc, x, Wk, bk, Wq, bq, Wv, bv, Wr, br, router_w, router_b, expert_w, expert_b,
                     const32, const_sel, const_eye, out):
    x_t = x.rearrange("b c h w -> b c (h w)").rearrange("b c (s i n) -> b s c i n", s=S, n=NT)
    o_t = out.rearrange("b c h w -> b c (h w)").rearrange("b c (s i n) -> b s c i n", s=S, n=NT)

    with ExitStack() as ctx:
        def sb(name, shape, dt=F32):
            return ctx.enter_context(nc.sbuf_tensor(name, shape, dt))

        def sem(name):
            return ctx.enter_context(nc.semaphore(name))

        widths = [P, P, P, P, 3, E, S, P, P]
        k32 = sb("k32", [P, sum(widths)])
        eye, centre, same_half, same_head, part_scale, first_wins, half_mean, bias_rows, add_halves = (
            k32[:, sum(widths[:i]):sum(widths[:i + 1])] for i in range(len(widths)))
        same_head, bias_rows = same_head[0:C, :], bias_rows[0:SE, :]
        sel = sb("sel", [P, CHUNKS, P], F16)
        eye16 = sb("eye16", [P, P], F16)
        w_nat = sb("w_nat", [P, 4, P])
        w_cen = sb("w_cen", [P, 3, P])
        w_mean = sb("w_mean", [P, 3])
        wk_bd = sb("wk_bd", [P, P])
        wq_bd = sb("wq_bd", [P, P])
        wvT = sb("wvT", [P, C])
        wrT = sb("wrT", [P, C])
        bk_row = sb("bk_row", [1, 4, C])
        bk_part = sb("bk_part", [1, 2, C], BF16)
        bk_rows = sb("bk_rows", [P, NT // C, C], BF16)
        ones16 = sb("ones16", [P, P], BF16)
        zeros16 = sb("zeros16", [P, P + 1], BF16)
        bq_col = sb("bq_col", [P, 1])
        br_col = sb("br_col", [P, 1])
        bv_row = sb("bv_row", [P, C])
        rb_row = sb("rb_row", [P, E])
        rw_nat = sb("rw_nat", [P, P])
        turn_route = sb("turn_route", [P, P + NLG])
        ew_nat = sb("ew_nat", [P, E // 2, C])
        ew = sb("ew", [P, E // 2, C])
        eb_in = sb("eb_in", [SE, P])
        eb_nat = sb("eb_nat", [P, P])
        eb_left = sb("eb_left", [P, 2, P])
        eb_part = sb("eb_part", [P, 3, P], BF16)
        eb_rows = sb("eb_rows", [P, P], BF16)

        xin = sb("xin", [P, 2, NT])
        xT = sb("xT", [P, 2, NT])
        sq = sb("sq", [P, 2, NT])
        stat = sb("stat", [P, 7, GR])
        xnT = sb("xnT", [P, 2, NJ, P + 1])
        xn = sb("xn", [P, 2, NT])
        keys = sb("keys", [P, 2, NT])
        kept = sb("kept", [P, TPB * NT])
        table_out = sb("table_out", [P, 1])
        s_sb = sb("s_sb", [P, P + 1])
        sT_sb = sb("sT_sb", [P, P])
        ctx_sb = sb("ctx_sb", [P, C])
        ctxT_sb = sb("ctxT_sb", [C, P])
        att = sb("att", [P, P])

        x_again = sb("x_again", [P, QUAD, NT])
        x1 = sb("x1", [P, 2, NT])
        sq_half = sb("sq_half", [P, 2, GR, C // 2])
        sq_quarter = sb("sq_quarter", [P, 2, GR, C // 4])
        lg = sb("lg", [P, TPB * NJ, NLG])
        ssq = sb("ssq", [P, TPB, GR])

        bstat = sb("bstat", [P, 5, TPB * GR])
        gstat = sb("gstat", [P, 6, QG])
        gl = sb("gl", [P, QG, E])
        gd = sb("gd", [P, 2, QG, E])
        gex = sb("gex", [P, QG, E])
        gk = sb("gk", [P, 2, QG, E])
        g2 = sb("g2", [P, QJ, 2, SE])
        gT = sb("gT", [P, QJ, P], F16)

        x1d = sb("x1d", [P, 2, S, NT])
        grows = sb("grows", [P, 2, NT], F16)
        gbs = sb("gbs", [P, PAIRS, NT])
        z = sb("z", [P, CHUNKS, NT])
        osb = sb("osb", [P, 2, NT])

        bank = [ctx.enter_context(nc.psum_tensor(f"bank{i}", [P, NT], F32)) for i in range(8)]
        bA, bB, bC, bD, bE, bF, bG, bH = bank
        attn_bank = [bB, bD]
        gb_bank = [[bC, bE], [bF, bG]]
        out_bank = [bH, bA]

        identity_in = sem("identity_in")
        const_in = sem("const_in")
        cleared = sem("cleared")
        keys_in = sem("keys_in")
        weights_in = sem("weights_in")
        weights_by_pool = sem("weights_by_pool")
        set_dve = sem("set_dve")
        set_pe = sem("set_pe")
        set_pool = sem("set_pool")
        bias_spread = sem("bias_spread")
        x_in = [sem(f"x_in{i}") for i in range(2)]
        x_again_in = [sem(f"x_again_in{i}") for i in range(QUAD)]
        xT_ready = sem("xT_ready")
        xT_copied = sem("xT_copied")
        xT_squared = sem("xT_squared")
        stat_own = sem("stat_own")
        norm_own = sem("norm_own")
        dev_root = sem("dev_root")
        norm_done = sem("norm_done")
        xn_ready = sem("xn_ready")
        xn_copied = sem("xn_copied")
        k_ready = sem("k_ready")
        k_done = sem("k_done")
        q_ready = sem("q_ready")
        q_done = sem("q_done")
        sum_done = sem("sum_done")
        fin_pe = sem("fin_pe")
        fin_dve = sem("fin_dve")
        attn_ready = sem("attn_ready")
        x1_done = sem("x1_done")
        x1_kept = sem("x1_kept")
        routed = sem("routed")
        x1_squared = sem("x1_squared")
        lg_copied = sem("lg_copied")
        half_summed = sem("half_summed")
        quarter_summed = sem("quarter_summed")
        ssq_done = sem("ssq_done")
        dev_done = sem("dev_done")
        gate_dve = sem("gate_dve")
        exp_done = sem("exp_done")
        high_done = sem("high_done")
        low_done = sem("low_done")
        x1d_in = [sem(f"x1d_in{i}") for i in range(2)]
        gT_ready = sem("gT_ready")
        grows_done = sem("grows_done")
        gb_ready = [sem(f"gb_ready{s}") for s in range(S)]
        gb_copied = sem("gb_copied")
        z_dve = sem("z_dve")
        z_pool = sem("z_pool")
        prod_done = sem("prod_done")
        out_done = sem("out_done")
        stored = [sem(f"stored{i}") for i in range(2)]

        credit = {norm_done: 2, sum_done: 2, q_ready: 2, routed: 4, x1_kept: 2, x1_done: 2, ssq_done: 2,
                  half_summed: 2, quarter_summed: 2, out_done: 2, grows_done: 2, xT_squared: 1,
                  xn_copied: 1, k_done: 1, q_done: 1, x1_squared: 1, lg_copied: 1, gT_ready: 1,
                  stored[0]: 16, stored[1]: 16, z_dve: PAIRS, gb_copied: PAIRS, z_pool: PAIRS, prod_done: CHUNKS,
                  gb_ready[0]: 2 * PAIRS, low_done: 2}
        credit = {s.name: n for s, n in credit.items()}
        N_FIN_PE, N_FIN_DVE, N_STAT, N_DEV, N_GATE = 4, 6, 9, 7, 20
        N_SET_CLEAR, N_SET_KQ, N_SET_V, N_SET_KEYS, N_SET_DVE = 3, 11, 14, 16, 23
        N_SET_BIAS, N_SET_POOL = 4, 14
        N_KEYS_IN, N_LOADS, N_POOL_LOADS = S * 2 + 1, S * 2 + 2, S * 4 + 1

        def done(eng, signal, n, more=0):
            eng.wait_ge(signal, n + (more + credit.get(signal.name, 0)))

        def give_credit(eng, *signals):
            for s in signals:
                eng.sem_inc(s, credit[s.name])

        z_done = [z_dve, z_pool]
        gates_read = [z_dve, gb_copied]

        block = ctx.enter_context(nc.Block())

        @block.sync
        def _(sp):
            def load_x(b, i, u):
                for s in range(S):
                    sp.dma_start(xin[C * s:C * s + C, u, :], x_t[b, s, :, i, :]).then_inc(x_in[u], 16)

            def load_again(b, i, k):
                for s in range(S):
                    sp.dma_start(x_again[C * s:C * s + C, k, :], x_t[b, s, :, i, :]).then_inc(x_again_in[k], 16)

            def spread(i, u):
                for s in range(S):
                    for d in range(2):
                        sp.dma_start(x1d[C * d:C * d + C, u, s, :],
                                     kept[C * s:C * s + C, bass.ds(i * NT, NT)]).then_inc(x1d_in[u], 16)

            def store(b, i, u):
                for s in range(S):
                    sp.dma_start(o_t[b, s, :, i, :], osb[C * s:C * s + C, u, :]).then_inc(stored[u], 16)

            give_credit(sp, *stored)
            sp.dma_start(k32[:, :], const32).then_inc(identity_in, 16)
            for u in range(2):
                load_x(0, u, u)
            sp.wait_ge(cleared, 1)
            for s in range(S):
                rows = slice(C * s, C * s + C)
                sp.dma_start(w_nat[rows, 0, rows], Wk).then_inc(keys_in, 16)
                sp.dma_start(w_nat[rows, 1, rows], Wq).then_inc(keys_in, 16)
            sp.dma_start(bk_row[0:1, 0, :], bk.rearrange("(a c) -> a c", a=1)).then_inc(keys_in, 16)
            for s in range(S):
                rows = slice(C * s, C * s + C)
                sp.dma_start(bq_col[rows, :], bq.rearrange("(c a) -> c a", a=1)).then_inc(weights_in, 16)
                sp.dma_start(br_col[rows, :], br.rearrange("(c a) -> c a", a=1)).then_inc(weights_in, 16)
            sp.dma_start(bv_row[:, :], bv.rearrange("(a c) -> a c", a=1).to_broadcast([P, C])).then_inc(weights_in, 16)
            sp.dma_start(rb_row[:, :], router_b.rearrange("(a c) -> a c", a=1).to_broadcast([P, E])
                         ).then_inc(weights_in, 16)
            sp.dma_start(sel[:, :, :].rearrange("p a b -> p (a b)"), const_sel).then_inc(const_in, 16)
            sp.dma_start(eye16[:, :], const_eye).then_inc(const_in, 16)

            def batch(b, has_next):
                with sp.Fori(0, TPB // 2 - 2) as pair:
                    i = 2 * pair + 2
                    for u in range(2):
                        done(sp, xT_ready, b * TPB + i + u + 1)
                        load_x(b, i + u + 2, u)
                for k in range(QUAD):
                    load_again(b, k, k)
                with sp.Fori(0, QUADS - 1) as q:
                    for k in range(QUAD):
                        done(sp, x1_done, b * TPB + q * QUAD + k + 1)
                        load_again(b, q * QUAD + k + QUAD, k)
                done(sp, x1_kept, b * TPB + 2)
                for u in range(2):
                    spread(u, u)
                done(sp, x1_kept, b * TPB + TPB)
                if has_next:
                    for u in range(2):
                        load_x(b + 1, u, u)
                with sp.Fori(0, TPB // 2 - 1) as pair:
                    i = 2 * pair
                    for u in range(2):
                        t = b * TPB + i + u
                        for s in range(S):
                            done(sp, z_done[s], t * PAIRS + PAIRS)
                        spread(i + u + 2, u)
                        done(sp, out_done, t + 1)
                        store(b, i + u, u)
                for u in range(2):
                    if has_next:
                        done(sp, xT_ready, b * TPB + TPB + u + 1)
                        load_x(b + 1, u + 2, u)
                    done(sp, out_done, b * TPB + TPB - 1 + u)
                    store(b, TPB - 2 + u, u)

            for u in range(2):
                done(sp, xT_ready, u + 1)
                load_x(0, u + 2, u)
            with sp.Fori(0, BATCH - 1) as b:
                batch(b, True)
            batch(BATCH - 1, False)
            for u in range(2):
                done(sp, stored[u], 16 * S * TILES // 2)

        def over_experts(a):
            return a.unsqueeze(2).to_broadcast([P, QG, E])

        def by_half(a):
            return a.rearrange("p (a s) e -> p a s e", s=S)

        def of_channels(a):
            return a.rearrange("p (g c) -> p g c", c=C)

        part_tiles = [slice(0, QUAD), slice(QUAD, 2 * QUAD), slice(2 * QUAD, TPB)]
        PARTS = len(part_tiles)

        def part_groups(part):
            return slice(part_tiles[part].start * GR, part_tiles[part].stop * GR)

        def gT_kinds(k0, copies):
            return gT[:, :, k0 * SE:(k0 + copies) * SE].rearrange("p a (k r) -> p a k r", k=copies)

        def gate_copies(kind, copies):
            return g2[:, :, kind, :].unsqueeze(2).to_broadcast([P, QJ, copies, SE])

        @block.gpsimd
        def _(pool):
            for tile in (w_nat, rw_nat, eb_in):
                pool.memset(tile[:], 0.0).then_inc(cleared, 1)
            give_credit(pool, z_pool, half_summed, quarter_summed)
            pool.wait_ge(cleared, 3)
            for s in range(S):
                rows = slice(C * s, C * s + C)
                pool.dma_start(w_nat[0:C, 2, rows], Wv).then_inc(weights_by_pool, 16)
                pool.dma_start(rw_nat[rows, E * s:E * s + E], router_w).then_inc(weights_by_pool, 16)
                pool.dma_start(ew_nat[rows, :, :], expert_w.rearrange("(p a) d c -> a d p c", a=2)[s]
                               ).then_inc(weights_by_pool, 16)
                pool.dma_start(eb_in[E * s:E * s + E, rows], expert_b).then_inc(weights_by_pool, 16)
            pool.dma_start(w_nat[0:C, 3, 0:C], Wr).then_inc(weights_by_pool, 16)

            n_set = [0]

            def then(ins):
                n_set[0] += 1
                ins.then_inc(set_pool, 1)
                pool.wait_ge(set_pool, n_set[0])

            pool.wait_ge(keys_in, 16 * N_KEYS_IN)
            then(pool.tensor_copy(bk_part[0:1, 0, :], bk_row[0:1, 0, :]))
            then(pool.tensor_tensor(bk_row[0:1, 1, :], bk_row[0:1, 0, :], bk_part[0:1, 0, :], ALU.subtract))
            then(pool.tensor_copy(bk_part[0:1, 1, :], bk_row[0:1, 1, :]))
            then(pool.tensor_tensor(bk_row[0:1, 2, :], bk_row[0:1, 1, :], bk_part[0:1, 1, :], ALU.subtract))
            assert n_set[0] == N_SET_BIAS
            pool.wait_ge(identity_in, 16)
            pool.wait_ge(set_dve, N_SET_DVE)
            then(pool.tensor_copy(eb_part[:, 0, :], eb_nat[:, :]))
            then(pool.tensor_tensor(eb_left[:, 0, :], eb_nat[:, :], eb_part[:, 0, :], ALU.subtract))
            then(pool.tensor_copy(eb_part[:, 1, :], eb_left[:, 0, :]))
            then(pool.tensor_tensor(eb_left[:, 1, :], eb_left[:, 0, :], eb_part[:, 1, :], ALU.subtract))
            then(pool.tensor_copy(eb_part[:, 2, :], eb_left[:, 1, :]))
            then(pool.tensor_scalar(eb_left[:, 0, :], eb_part[:, 0, :], part_scale[:, 0:1], None, ALU.mult))
            then(pool.tensor_scalar(eb_left[:, 1, :], eb_part[:, 1, :], part_scale[:, 1:2], None, ALU.mult))
            then(pool.tensor_tensor(eb_left[:, 0, :], eb_left[:, 0, :], eb_left[:, 1, :], ALU.add))
            then(pool.tensor_scalar(eb_left[:, 1, :], eb_part[:, 2, :], part_scale[:, 2:3], None, ALU.mult))
            then(pool.tensor_tensor(eb_rows[:, :], eb_left[:, 0, :], eb_left[:, 1, :], ALU.add))
            assert n_set[0] == N_SET_POOL

            def products(b, i, u):
                t = b * TPB + i + u
                pool.wait_ge(x1d_in[u], b * (32 * TPB) + i * 32 + 64)
                for j in range(PAIRS):
                    c = j * S + 1
                    done(pool, gb_copied, t * PAIRS + j + 1)
                    done(pool, prod_done, t * CHUNKS, c + 1 - CHUNKS)
                    pool.tensor_tensor(z[:, c, :], gbs[:, j, :], x1d[:, u, 1, :], ALU.mult).then_inc(z_pool, 1)

            with pool.Fori(0, BATCH) as b:
                with pool.Fori(0, TPB // 2) as pair:
                    for u in range(2):
                        t = b * TPB + 2 * pair + u
                        done(pool, x1_squared, t + 1)
                        done(pool, quarter_summed, t, -1)
                        pool.tensor_tensor(sq_half[:, u], of_channels(sq[:, u, :])[:, :, 0:C // 2],
                                           of_channels(sq[:, u, :])[:, :, C // 2:C], ALU.add).then_inc(half_summed, 1)
                        done(pool, half_summed, t + 1)
                        done(pool, ssq_done, t, -1)
                        pool.tensor_tensor(sq_quarter[:, u], sq_half[:, u, :, 0:C // 4],
                                           sq_half[:, u, :, C // 4:C // 2], ALU.add).then_inc(quarter_summed, 1)
                with pool.Fori(0, TPB // 2) as pair:
                    for u in range(2):
                        products(b, 2 * pair, u)

        @block.scalar
        def _(act):
            give_credit(act, x1_kept, grows_done, gb_copied, xT_squared, xn_copied, k_done, q_done, x1_squared,
                        low_done)

            def take_x(t, u):
                act.wait_ge(xT_ready, t + 1)
                done(act, norm_done, t, -1)
                nc.scalar.copy(xT[:, u, :], bD[:, :]).then_inc(xT_copied, 1)
                nc.scalar.activation(sq[:, u, :], bD[:, :], ACT.Square, scale=C ** -0.5).then_inc(xT_squared, 1)

            def root(t):
                act.wait_ge(stat_own, t * N_STAT + 6)
                nc.scalar.activation(stat[:, 6, :], stat[:, 3, :], ACT.Sqrt).then_inc(norm_own, 1)

            def take_xn(t, u):
                act.wait_ge(xn_ready, t + 1)
                done(act, q_ready, t, -1)
                nc.scalar.copy(xn[:, u, :], bB[:, :]).then_inc(xn_copied, 1)

            def batch(b, has_next):
                t0 = b * TPB

                def take_keys(t, u):
                    act.wait_ge(k_ready, t + 1)
                    done(act, sum_done, t, -1)
                    nc.scalar.activation(keys[:, u, :], bC[:, :], ACT.Relu).then_inc(k_done, 1)

                def take_queries(i, u):
                    done(act, q_ready, t0 + i + u + 1)
                    nc.scalar.activation(kept[:, bass.ds((i + u) * NT, NT)], bH[:, :], ACT.Relu,
                                         bias=bq_col[:, 0:1]).then_inc(q_done, 1)

                with act.Fori(0, TPB // 2 - 1) as pair:
                    i = 2 * pair
                    for u in range(2):
                        take_x(t0 + i + u + 2, u)
                        take_keys(t0 + i + u, u)
                        take_queries(i, u)
                        root(t0 + i + u + 2)
                        take_xn(t0 + i + u + 1, 1 - u)
                take_keys(t0 + TPB - 2, 0)
                take_xn(t0 + TPB - 1, 1)
                take_keys(t0 + TPB - 1, 1)
                take_queries(TPB - 2, 0)
                take_queries(TPB - 2, 1)

                def keep(i, u):
                    t = t0 + i + u
                    done(act, x1_done, t + 1)
                    done(act, attn_ready, t + 1)
                    nc.scalar.copy(kept[:, bass.ds((i + u) * NT, NT)], x1[:, u, :]).then_inc(x1_kept, 1)
                    done(act, half_summed, t, -1)
                    for k, half in enumerate((bA, bC)):
                        done(act, routed, 2 * t + k + 1)
                        both = half[:, 0:2 * (P + NLG)].rearrange("p (j n) -> p j n", j=2)
                        squares = sq[:, u, 2 * k * P:2 * (k + 1) * P].rearrange("p (j n) -> p j n", j=2)
                        ins = nc.scalar.activation(squares, both[:, :, 0:P], ACT.Square, scale=C ** -0.5)
                        if k == 1:
                            ins.then_inc(x1_squared, 1)
                        ins = nc.scalar.copy(lg[:, bass.ds((i + u) * NJ + 2 * k, 2), :], both[:, :, P:P + NLG])
                    ins.then_inc(lg_copied, 1)

                def dev_roots(part):
                    g = part_groups(part)
                    n = PARTS * b + part
                    act.wait_ge(dev_done, n * N_DEV + 4)
                    nc.scalar.activation(bstat[:, 4, g], bstat[:, 0, g], ACT.Sqrt).then_inc(dev_root, 1)

                def exponent(q):
                    n = b * QUADS + q
                    act.wait_ge(gate_dve, n * N_GATE + 9)
                    nc.scalar.activation(gex[:, :, :], gd[:, 0], ACT.Exp).then_inc(exp_done, 1)
                    nc.scalar.activation(gstat[:, 5, :], gstat[:, 2, :], ACT.Exp).then_inc(exp_done, 1)

                def high(q):
                    n = b * QUADS + q
                    act.wait_ge(gate_dve, n * N_GATE + 19)
                    done(act, gT_ready, n * (QUAD // 2))
                    for kind, k0, copies in ((0, 0, 1), (1, 2, 3)):
                        nc.scalar.copy(gT_kinds(k0, copies), gate_copies(kind, copies)).then_inc(high_done, 1)

                def low(q):
                    n = b * QUADS + q
                    act.wait_ge(gate_dve, n * N_GATE + 20)
                    for kind, k0, copies in ((0, 1, 1), (1, 5, 3)):
                        nc.scalar.activation(gT_kinds(k0, copies), gate_copies(kind, copies), ACT.Copy,
                                             scale=1.0 / LO).then_inc(low_done, 1)

                def gate_rows(h, u):
                    t = t0 + h * 2 + u
                    done(act, gT_ready, b * (TPB // 2) + h + 1)
                    done(act, gb_ready[0], t * PAIRS, -PAIRS)
                    nc.scalar.copy(grows[:, u, :], bB[:, u * (NT // 2):(u + 1) * (NT // 2)].bitcast(F16)
                                   ).then_inc(grows_done, 1)

                def copy_gates(t, *js):
                    for j in js:
                        act.wait_ge(gb_ready[1], t * PAIRS + j + 1)
                        done(act, z_pool, t * PAIRS, j + 1 - PAIRS)
                        nc.scalar.copy(gbs[:, j, :], gb_bank[1][j % 2][:, :]).then_inc(gb_copied, 1)

                with act.Fori(0, QUAD // 2) as pair:
                    for u in range(2):
                        keep(2 * pair, u)
                beside = {QUAD: lambda: dev_roots(0), 2 * QUAD + 1: lambda: exponent(0), TPB - 5: lambda: dev_roots(1),
                          TPB - 4: lambda: high(0), TPB - 3: lambda: low(0)}
                for i in range(QUAD, TPB - 1):
                    keep(i - i % 2, i % 2)
                    if i in beside:
                        beside[i]()
                gate_rows(0, 0)
                gate_rows(0, 1)
                keep(TPB - 2, 1)
                copy_gates(t0, 0, 1)
                dev_roots(2)
                nc.scalar.activation(table_out[:, :], bq_col[:, :], ACT.Exp, scale=0.0)

                def pair_of_tiles(h, first=lambda: None, second=lambda: None, third=lambda: None,
                                  fourth=lambda: None):
                    t = t0 + h * 2
                    copy_gates(t, 2, 3)
                    first()
                    copy_gates(t + 1, 0, 1)
                    second()
                    copy_gates(t + 1, 2)
                    third()
                    gate_rows(h + 1, 0)
                    copy_gates(t + 1, 3)
                    fourth()
                    copy_gates(t + 2, 0, 1)
                    gate_rows(h + 1, 1)

                with act.Fori(0, QUADS - 1) as q:
                    pair_of_tiles(2 * q, third=lambda: exponent(q + 1))
                    pair_of_tiles(2 * q + 1, first=lambda: high(q + 1), second=lambda: low(q + 1))
                h, t, n = TPB // 2 - 2, t0 + TPB - 2, t0 + TPB
                if not has_next:
                    pair_of_tiles(h)
                    copy_gates(t, 2, 3)
                    copy_gates(t + 1, 0, 1, 2, 3)
                else:
                    pair_of_tiles(h, second=lambda: take_x(n, 0), fourth=lambda: root(n))
                    take_x(n + 1, 1)
                    copy_gates(t, 2, 3)
                    copy_gates(t + 1, 0)
                    root(n + 1)
                    copy_gates(t + 1, 1, 2)
                    take_xn(n, 0)
                    copy_gates(t + 1, 3)

            take_x(0, 0)
            root(0)
            take_x(1, 1)
            take_xn(0, 0)
            root(1)
            act.wait_ge(set_pool, N_SET_BIAS)
            act.wait_ge(set_dve, N_SET_CLEAR)
            for k in range(3):
                nc.scalar.copy(bk_rows[32 * k:32 * k + 1, :, :],
                               bk_row[0:1, k, :].unsqueeze(1).to_broadcast([1, NT // C, C])).then_inc(bias_spread, 1)
            act.wait_ge(weights_in, 16 * N_LOADS)
            with act.Fori(0, BATCH - 1) as b:
                batch(b, True)
            batch(BATCH - 1, False)

        @block.vector
        def _(dve):
            n_set = [0]

            def then(ins, wait=True):
                n_set[0] += 1
                ins.then_inc(set_dve, 1)
                if wait:
                    dve.wait_ge(set_dve, n_set[0])

            def newton(out, root, variance, work):
                return [lambda: dve.scalar_tensor_tensor(work[0], root, -0.5, root, ALU.mult, ALU.mult),
                        lambda: dve.tensor_tensor(work[1], work[0], variance, ALU.mult),
                        lambda: dve.scalar_tensor_tensor(out, work[1], 1.5, root, ALU.add, ALU.mult)]

            def sum_x(t, u):
                own = t * N_STAT
                dve.wait_ge(xT_copied, t + 1)
                dve.tensor_reduce(stat[:, 0, :], xT[:, u, :].rearrange("p (g c) -> p g c", c=C),
                                  AX_X, ALU.add).then_inc(stat_own, 1)
                dve.wait_ge(stat_own, own + 1)
                dve.scalar_tensor_tensor(stat[:, 1, :], stat[:, 0, :], 1.0 / C ** 2, stat[:, 0, :],
                                         ALU.mult, ALU.mult).then_inc(stat_own, 1)

            def vary_x(t, u):
                own = t * N_STAT
                done(dve, xT_squared, t + 1)
                dve.tensor_reduce(stat[:, 2, :], sq[:, u, :].rearrange("p (g c) -> p g c", c=C),
                                  AX_X, ALU.add).then_inc(stat_own, 1)
                dve.wait_ge(stat_own, own + 3)
                dve.tensor_tensor(stat[:, 3, :], stat[:, 2, :], stat[:, 1, :], ALU.subtract).then_inc(stat_own, 1)
                dve.wait_ge(stat_own, own + 4)
                dve.tensor_scalar(stat[:, 4, :], stat[:, 3, :], 0.0, EPS_CONV, ALU.max, ALU.add).then_inc(stat_own, 1)
                dve.wait_ge(stat_own, own + 5)
                dve.reciprocal(stat[:, 3, :], stat[:, 4, :]).then_inc(stat_own, 1)

            def measure_x(t, u):
                sum_x(t, u)
                vary_x(t, u)

            def normalise(t, u):
                own = t * N_STAT
                dve.wait_ge(norm_own, t + 1)
                steps = newton(stat[:, 5, :], stat[:, 6, :], stat[:, 4, :], (stat[:, 0, :], stat[:, 1, :]))
                for k, step in enumerate(steps):
                    if k:
                        dve.wait_ge(stat_own, own + 6 + k)
                    step().then_inc(stat_own, 1)
                dve.wait_ge(stat_own, own + N_STAT)
                done(dve, sum_done, t, -1)
                dve.tensor_tensor(xnT[:, u, :, 0:P].rearrange("p j (s c) -> p j s c", s=S),
                                  xT[:, u, :].rearrange("p (j s c) -> p j s c", j=NJ, s=S),
                                  stat[:, 5, :].rearrange("p (j s) -> p j s", s=S).unsqueeze(3)
                                  .to_broadcast([P, NJ, S, C]), ALU.mult).then_inc(norm_done, 1)

            give_credit(dve, norm_done, x1_done, ssq_done, out_done, z_dve, lg_copied)
            then(dve.memset(ones16[:, :], 1.0), False)
            then(dve.memset(zeros16[:, :], 0.0), False)
            then(dve.memset(bk_rows[:, :, :], 0.0), False)
            assert n_set[0] == N_SET_CLEAR
            then(dve.memset(xnT[:, :, :, :], 1.0), False)
            then(dve.memset(att[:, :], 0.0))
            for u in range(2):
                measure_x(u, u)
                normalise(u, u)
            dve.wait_ge(identity_in, 16)

            def less_mean(k, rows, width):
                then(dve.tensor_reduce(w_mean[0:rows, k:k + 1], w_nat[0:rows, k, 0:width], AX_X, ALU.add))
                then(dve.tensor_scalar(w_mean[0:rows, k:k + 1], w_mean[0:rows, k:k + 1], -1.0 / C, None, ALU.mult))
                if k < 2:
                    then(dve.scalar_tensor_tensor(w_cen[:, k, :], same_half, w_mean[:, k:k + 1], w_nat[:, k, :],
                                                  ALU.mult, ALU.add))
                else:
                    then(dve.tensor_scalar(w_cen[0:C, k, :], w_nat[0:C, k, :], w_mean[0:C, k:k + 1], None, ALU.add))

            dve.wait_ge(keys_in, 16 * N_KEYS_IN)
            less_mean(0, P, P)
            less_mean(1, P, P)
            assert n_set[0] == N_SET_KQ
            dve.wait_ge(weights_in, 16 * N_LOADS)
            dve.wait_ge(weights_by_pool, 16 * N_POOL_LOADS)
            less_mean(2, C, C)
            assert n_set[0] == N_SET_V
            dve.wait_ge(set_pe, 1)
            then(dve.tensor_copy(wk_bd[:, :], bH[:, 0:P]), False)
            then(dve.tensor_copy(wq_bd[:, :], bH[:, P:2 * P]))
            assert n_set[0] == N_SET_KEYS
            dve.wait_ge(set_pe, 2)
            then(dve.tensor_copy(wvT[:, :], bG[:, 0:C]), False)
            then(dve.tensor_copy(wrT[0:C, :], bG[0:C, C:P]), False)
            then(dve.tensor_copy(ew[:, :, :].rearrange("p a c -> p (a c)"), bF[:, 0:E // 2 * C]), False)
            then(dve.tensor_copy(turn_route[:, 0:P], eye), False)
            then(dve.tensor_copy(turn_route[:, P:P + SE], bA[:, P:P + SE]), False)
            then(dve.tensor_copy(turn_route[:, P + SE:P + NLG], half_mean), False)
            then(dve.tensor_copy(eb_nat[:, :], bA[:, 0:P]))
            assert n_set[0] == N_SET_DVE

            def batch(b, has_next):
                t0 = b * TPB

                with dve.Fori(0, TPB // 2 - 1) as pair:
                    for u in range(2):
                        t = t0 + 2 * pair + u + 2
                        measure_x(t, u)
                        normalise(t, u)

                dve_f, pe_f = b * N_FIN_DVE, b * N_FIN_PE
                done(dve, sum_done, t0 + TPB)
                dve.tensor_copy(s_sb[:, :], bE[:, 0:P + 1]).then_inc(fin_dve, 1)
                dve.wait_ge(fin_pe, pe_f + 1)
                dve.tensor_tensor(sT_sb[:, :], bF[:, 0:P], same_half, ALU.mult).then_inc(fin_dve, 1)
                dve.wait_ge(fin_pe, pe_f + 2)
                dve.scalar_tensor_tensor(ctx_sb[:, :], bv_row[:, :], s_sb[:, P:P + 1], bG[:, 0:C],
                                         ALU.mult, ALU.add).then_inc(fin_dve, 1)
                dve.wait_ge(fin_pe, pe_f + 3)
                dve.tensor_tensor(ctxT_sb[:, :], bF[0:C, 0:P], same_head, ALU.mult).then_inc(fin_dve, 1)
                dve.wait_ge(fin_pe, pe_f + 4)
                dve.tensor_copy(att[0:C, 0:C], bG[0:C, 0:C]).then_inc(fin_dve, 1)
                dve.tensor_copy(att[C:P, C:P], bG[C:P, 0:C]).then_inc(fin_dve, 1)

                def residual(i):
                    t, u, k = t0 + i, i % 2, i % QUAD
                    dve.wait_ge(attn_ready, t + 1)
                    dve.wait_ge(x_again_in[k], b * (32 * QUADS) + (i // QUAD * 32 + 32))
                    done(dve, routed, 2 * t, -2)
                    done(dve, x1_kept, t, -1)
                    dve.scalar_tensor_tensor(x1[:, u, :], attn_bank[u][:, :], br_col[:, 0:1], x_again[:, k, :],
                                             ALU.add, ALU.add).then_inc(x1_done, 1)

                def measure(t, i, u, *between):
                    for step in between[0:1]:
                        step()
                    done(dve, quarter_summed, t + 1)
                    dve.tensor_reduce(ssq[:, i + u, :], sq_quarter[:, u], AX_X, ALU.add).then_inc(ssq_done, 1)
                    for step in between[1:]:
                        step()

                def deviations(part):
                    g = part_groups(part)
                    tiles = part_tiles[part]
                    n = PARTS * b + part
                    mean = lg[:, tiles.start * NJ:tiles.stop * NJ, SE:NLG]
                    k = [0]

                    def step(fn):
                        def run():
                            if k[0] == 4:
                                dve.wait_ge(dev_root, n + 1)
                            elif k[0]:
                                dve.wait_ge(dev_done, n * N_DEV + k[0])
                            else:
                                done(dve, ssq_done, t0 + tiles.stop)
                                done(dve, lg_copied, t0 + tiles.stop)
                            k[0] += 1
                            fn().then_inc(dev_done, 1)
                        return run

                    steps = [
                        lambda: dve.tensor_tensor(bstat[:, 0, g].rearrange("p (a s) -> p a s", s=S), mean, mean,
                                                  ALU.mult),
                        lambda: dve.tensor_tensor(bstat[:, 1, g], ssq[:, tiles, :].rearrange("p t g -> p (t g)"),
                                                  bstat[:, 0, g], ALU.subtract),
                        lambda: dve.tensor_scalar(bstat[:, 2, g], bstat[:, 1, g], 0.0, EPS_FFN, ALU.max, ALU.add),
                        lambda: dve.reciprocal(bstat[:, 0, g], bstat[:, 2, g]),
                        *newton(bstat[:, 3, g], bstat[:, 4, g], bstat[:, 2, g], (bstat[:, 1, g], bstat[:, 0, g]))]
                    assert len(steps) == N_DEV
                    return [step(fn) for fn in steps]

                def gate_steps(q, part, issued=0):
                    n = b * QUADS + q
                    own = n * N_GATE
                    first = first_wins.unsqueeze(1).to_broadcast([P, QG, E])
                    kinds = g2[:, :, :, :].rearrange("p a k (s e) -> p a k s e", s=S)
                    over_dev = by_half(over_experts(bstat[:, 3, bass.ds(q * QG, QG)]))
                    k = [issued]

                    def step(fn):
                        def run():
                            if k[0]:
                                dve.wait_ge(gate_dve, own + k[0])
                            k[0] += 1
                            fn().then_inc(gate_dve, 1)
                        return run

                    def choose():
                        dve.wait_ge(exp_done, n * 2 + 2)
                        return dve.tensor_tensor(gl[:, :, :], gex[:, :, :], gk[:, 0], ALU.mult)

                    def gate():
                        done(dve, low_done, n * 2)
                        return dve.tensor_tensor(kinds[:, :, 1], by_half(gl[:, :, :]),
                                                 by_half(over_experts(gstat[:, 4, :])), ALU.mult)

                    def left():
                        dve.wait_ge(high_done, n * 2 + 2)
                        return dve.tensor_tensor(g2[:, :, :, :], g2[:, :, :, :],
                                                 gT[:, :, :].rearrange("p a (k r) -> p a k r", r=SE)[:, :, 0:3:2, :],
                                                 ALU.subtract)

                    def scale():
                        dve.wait_ge(dev_done, (PARTS * b + part) * N_DEV + N_DEV)
                        return dve.tensor_tensor(by_half(gl[:, :, :]),
                                                 lg[:, bass.ds(q * QJ, QJ), 0:SE]
                                                 .rearrange("p a (s e) -> p a s e", s=S), over_dev, ALU.mult)

                    def tied(j):
                        return lambda: dve.scalar_tensor_tensor(gk[:, j], gd[:, j], 0.0, first, ALU.is_ge, ALU.mult)

                    def lowest(j):
                        return lambda: dve.tensor_reduce(gstat[:, 1, :], gk[:, j], AX_X, ALU.max)

                    def mask(j):
                        return lambda: dve.tensor_tensor(gk[:, j], gk[:, j], over_experts(gstat[:, 1, :]),
                                                         ALU.is_equal)

                    steps = [
                        scale,
                        lambda: dve.tensor_tensor(gl[:, :, :], gl[:, :, :],
                                                  rb_row[:, :].unsqueeze(1).to_broadcast([P, QG, E]), ALU.add),
                        lambda: dve.tensor_reduce(gstat[:, 0, :], gl[:, :, :], AX_X, ALU.max),
                        lambda: dve.tensor_tensor(gd[:, 0], gl[:, :, :], over_experts(gstat[:, 0, :]), ALU.subtract),
                        tied(0), lowest(0), mask(0),
                        lambda: dve.scalar_tensor_tensor(gd[:, 1], gk[:, 0], -BIG, gd[:, 0], ALU.mult, ALU.add),
                        lambda: dve.tensor_reduce(gstat[:, 2, :], gd[:, 1], AX_X, ALU.max),
                        lambda: dve.tensor_tensor(gd[:, 1], gd[:, 1], over_experts(gstat[:, 2, :]), ALU.subtract),
                        tied(1), lowest(1), mask(1),
                        lambda: dve.tensor_tensor(gk[:, 0], gk[:, 0], gk[:, 1], ALU.add),
                        choose,
                        lambda: dve.tensor_scalar(gstat[:, 3, :], gstat[:, 5, :], 1.0, None, ALU.add),
                        lambda: dve.reciprocal(gstat[:, 4, :], gstat[:, 3, :]),
                        gate,
                        lambda: dve.tensor_tensor(kinds[:, :, 0], kinds[:, :, 1], over_dev, ALU.mult),
                        left]
                    assert len(steps) == N_GATE
                    return [step(fn) for fn in steps]

                def product(h, u, j, *between):
                    t = t0 + h * 2 + u
                    if j == 0:
                        dve.wait_ge(x1d_in[u], b * (32 * TPB) + h * 64 + 64)
                    c = j * S
                    done(dve, gb_ready[0], t * PAIRS + j + 1)
                    done(dve, prod_done, t * CHUNKS, c + 1 - CHUNKS)
                    dve.tensor_tensor(z[:, c, :], gb_bank[0][j % 2][:, :], x1d[:, u, 0, :],
                                      ALU.mult).then_inc(z_dve, 1)
                    for step in between:
                        step()

                def result(h, u, *between):
                    t = t0 + h * 2 + u
                    done(dve, prod_done, t * CHUNKS + CHUNKS)
                    done(dve, stored[u], b * (16 * TPB) + h * 32)
                    dve.tensor_tensor(osb[:, u, :], out_bank[u][:, :], kept[:, bass.ds(h * (2 * NT) + u * NT, NT)],
                                      ALU.add).then_inc(out_done, 1)
                    for step in between:
                        step()

                def rest_of_tile(h, u, steps):
                    product(h, u, 2, *steps[0])
                    product(h, u, 3, *steps[1])
                    product(h + u, 1 - u, 0, *steps[2])
                    result(h, u, *steps[3])
                    product(h + u, 1 - u, 1, *steps[4])

                residual(0)
                residual(1)
                for i in range(QUAD):
                    residual(i + 2)
                    measure(t0 + i, i - i % 2, i % 2)
                first, second, others = (deviations(part) for part in range(PARTS))
                g, f = gate_steps(0, 0), gate_steps(1, 1)[0:AHEAD_STEPS]
                for step in first[0:4]:
                    step()
                between = [first[4:] + g[0:1], g[1:4], g[4:7], g[7:10], g[10:13], second[0:4] + g[13:14],
                           g[14:17], g[17:19] + second[4:5], second[5:] + g[19:], f[0:3], f[3:]]
                assert len(between) == TPB - QUAD - 1
                for i in range(QUAD, TPB - 1):
                    if i + 2 < TPB:
                        residual(i + 2)
                    measure(t0 + i, i - i % 2, i % 2, *between[i - QUAD])

                product(0, 0, 0)
                measure(t0 + TPB - 1, TPB - 2, 1)
                for step in others[0:4]:
                    step()
                product(0, 0, 1, *others[4:])

                def quad(q, now, ahead):
                    g = [now[0:1], now[1:2], now[2:3], [], now[3:4]]
                    rest_of_tile(2 * q, 0, g)
                    g = [now[4:5], now[5:7], now[7:8], now[8:9], now[9:10]]
                    rest_of_tile(2 * q, 1, g)
                    g = [now[10:12], now[12:13], now[13:14], [], []]
                    rest_of_tile(2 * q + 1, 0, g)
                    g = [ahead[0:1], ahead[1:3], ahead[3:4], ahead[4:5], ahead[5:6]]
                    rest_of_tile(2 * q + 1, 1, g)

                with dve.Fori(0, QUADS - 2) as q:
                    quad(q, gate_steps(q + 1, 1, AHEAD_STEPS)[AHEAD_STEPS:], gate_steps(q + 2, 2))
                quad(QUADS - 2, gate_steps(QUADS - 1, 1, AHEAD_STEPS)[AHEAD_STEPS:], [])
                h, n = TPB // 2 - 1, t0 + TPB

                def next_x(fn, u):
                    return [lambda: fn(n + u, u)] if has_next else []

                rest_of_tile(h - 1, 0, [[], [], [], [], next_x(sum_x, 0)])
                rest_of_tile(h - 1, 1, [next_x(vary_x, 0), [], next_x(normalise, 0), [], next_x(sum_x, 1)])
                rest_of_tile(h, 0, [next_x(vary_x, 1), [], [], next_x(normalise, 1), []])
                product(h, 1, 2)
                product(h, 1, 3)
                result(h, 1)

            with dve.Fori(0, BATCH - 1) as b:
                batch(b, True)
            batch(BATCH - 1, False)

        @block.tensor
        def _(pe):
            give_credit(pe, sum_done, q_ready, routed, prod_done, gT_ready, gb_ready[0])

            def turn_x(b, h, u):
                pe.wait_ge(x_in[u], b * (16 * TPB) + h * 32 + 32)
                done(pe, xT_squared, b * TPB + h * 2 + u)
                for j in range(NJ):
                    ins = pe.transpose(bD[:, j * P:(j + 1) * P], xin[:, u, j * P:(j + 1) * P], eye)
                ins.then_inc(xT_ready, 1)

            def turn_back(t, u):
                done(pe, norm_done, t + 1)
                done(pe, xn_copied, t)
                for j in range(NJ):
                    ins = pe.transpose(bB[:, j * P:(j + 1) * P], xnT[:, u, j, 0:P], eye)
                ins.then_inc(xn_ready, 1)

            def batch(b, has_next):
                t0 = b * TPB

                def make_keys(t, u):
                    done(pe, xn_copied, t + 1)
                    done(pe, k_done, t)
                    pe.matmul(bC[:, :], ones16[:, :], bk_rows[:, :, :].rearrange("p g c -> p (g c)"),
                              start=True, stop=False, skip_group_check=True)
                    for j in range(NJ):
                        ins = pe.matmul(bC[:, j * P:(j + 1) * P], xn[:, u, j * P:(j + 1) * P], wk_bd[:, :],
                                        start=False, stop=(j == NJ - 1), skip_group_check=True)
                    ins.then_inc(k_ready, 1)

                def make_queries(t, u):
                    done(pe, q_done, t)
                    pe.matmul(bH[:, :], wq_bd[:, :], xn[:, u, :], start=True, stop=True).then_inc(q_ready, 1)

                def sums(t, u, last):
                    done(pe, k_done, t + 1)
                    for j in range(NJ):
                        ins = pe.matmul(bE[:, 0:P + 1], keys[:, u, j * P:(j + 1) * P], xnT[:, u, j, :],
                                        start=False, stop=(last and j == NJ - 1), skip_group_check=True)
                    ins.then_inc(sum_done, 1)

                done(pe, out_done, t0, -1)
                pe.matmul(bE[:, 0:P + 1], ones16[:, :], zeros16[:, :], start=True, stop=False, skip_group_check=True)
                with pe.Fori(0, TPB // 2 - 1) as pair:
                    i = 2 * pair
                    for u in range(2):
                        t = t0 + i + u
                        turn_x(b, pair + 1, u)
                        make_keys(t, u)
                        make_queries(t, u)
                        turn_back(t + 1, 1 - u)
                        sums(t, u, False)
                t = t0 + TPB - 2
                make_keys(t, 0)
                turn_back(t + 1, 1)
                sums(t, 0, False)
                make_keys(t + 1, 1)
                make_queries(t, 0)
                sums(t + 1, 1, True)
                make_queries(t + 1, 1)

                dve_f = b * N_FIN_DVE
                pe.wait_ge(set_dve, N_SET_DVE)
                pe.wait_ge(set_pool, N_SET_POOL)
                pe.wait_ge(const_in, 16 * 2)
                pe.wait_ge(fin_dve, dve_f + 1)
                pe.transpose(bF[:, 0:P], s_sb[:, 0:P], eye).then_inc(fin_pe, 1)
                pe.wait_ge(fin_dve, dve_f + 2)
                pe.matmul(bG[:, 0:C], sT_sb[:, :], wvT[:, :], start=True, stop=True).then_inc(fin_pe, 1)
                pe.wait_ge(fin_dve, dve_f + 3)
                pe.matmul(bF[0:C, 0:P], ctx_sb[:, :], add_halves, start=True, stop=True).then_inc(fin_pe, 1)
                pe.wait_ge(fin_dve, dve_f + 4)
                pe.matmul(bG[:, 0:C], ctxT_sb[:, :], wrT[0:C, :], start=True, stop=True).then_inc(fin_pe, 1)
                pe.wait_ge(fin_dve, dve_f + 6)

                def attend(t, i, u):
                    done(pe, x1_done, t, -1)
                    pe.matmul(attn_bank[u][:, :], att[:, :], kept[:, bass.ds(i * NT, NT)],
                              start=True, stop=True).then_inc(attn_ready, 1)

                def route(t, u):
                    done(pe, x1_done, t + 1)
                    done(pe, x1_squared, t)
                    done(pe, lg_copied, t)
                    for j in range(NJ):
                        half, k = (bA, bC)[j // 2], j % 2 * (P + NLG)
                        ins = pe.matmul(half[:, k:k + P + NLG], x1[:, u, j * P:(j + 1) * P], turn_route[:, :],
                                        start=True, stop=True)
                        if j % 2 == 1:
                            ins.then_inc(routed, 1)

                done(pe, q_done, t0 + TPB)
                done(pe, out_done, t0)
                attend(t0, 0, 0)
                with pe.Fori(0, TPB // 2 - 1) as pair:
                    i = 2 * pair
                    for u in range(2):
                        attend(t0 + i + u + 1, i + u + 1, 1 - u)
                        route(t0 + i + u, u)
                attend(t0 + TPB - 1, TPB - 1, 1)
                route(t0 + TPB - 2, 0)

                def turn_gates(h, odd):
                    if not odd:
                        done(pe, low_done, b * (2 * QUADS) + h + 2)
                    done(pe, grows_done, t0 + h * 2)
                    for j in range(2 * NJ):
                        ins = pe.transpose(bB[:, j * C:(j + 1) * C].bitcast(F16), gT[:, 2 * NJ * odd + j, :],
                                           eye16[:, :])
                    ins.then_inc(gT_ready, 1)

                def broadcast(t, u, j, s):
                    if s == 1 and j == 0:
                        done(pe, grows_done, t + 1)
                    done(pe, gates_read[s], t * PAIRS, j - 1)
                    pe.matmul(gb_bank[s][j % 2][:, :], sel[:, j * S + s, :], grows[:, u, :],
                              start=True, stop=True).then_inc(gb_ready[s], 1)

                def experts(h, u, has_next=True, beside={}):
                    t = t0 + h * 2 + u
                    done(pe, out_done, t, -1)
                    pe.matmul(out_bank[u][:, :], eb_rows[:, :], grows[:, u, :], start=True, stop=False,
                              skip_group_check=True)
                    for j in range(PAIRS):
                        if j in beside:
                            beside[j]()
                        for s in (1, 0):
                            if j + AHEAD < PAIRS:
                                broadcast(t, u, j + AHEAD, s)
                            elif has_next:
                                broadcast(t + 1, 1 - u, j + AHEAD - PAIRS, s)
                        for s in range(S):
                            done(pe, z_done[s], t * PAIRS + j + 1)
                            pe.matmul(out_bank[u][C * s:C * s + C, :], ew[:, j, :], z[:, j * S + s, :], start=False,
                                      stop=(j == PAIRS - 1), skip_group_check=True).then_inc(prod_done, 1)

                done(pe, x1_done, t0 + TPB)
                turn_gates(0, 0)
                route(t0 + TPB - 1, 1)
                for j in range(AHEAD):
                    broadcast(t0, 0, j, 1)
                done(pe, x1_squared, t0 + TPB)
                done(pe, lg_copied, t0 + TPB)
                for j in range(AHEAD):
                    broadcast(t0, 0, j, 0)
                with pe.Fori(0, QUADS - 1) as q:
                    for odd in range(2):
                        h = 2 * q + odd
                        experts(h, 0)
                        experts(h, 1, beside={1: lambda: turn_gates(h + 1, 1 - odd)})
                h = TPB // 2 - 1
                if has_next:
                    experts(h - 1, 0, beside={2: lambda: turn_x(b + 1, 0, 0)})
                    experts(h - 1, 1, beside={1: lambda: turn_gates(h, 1), 3: lambda: turn_x(b + 1, 0, 1)})
                    experts(h, 0)
                    experts(h, 1, False, beside={1: lambda: turn_back(t0 + TPB, 0)})
                else:
                    experts(h - 1, 0)
                    experts(h - 1, 1, beside={1: lambda: turn_gates(h, 1)})
                    experts(h, 0)
                    experts(h, 1, False)

            pe.wait_ge(identity_in, 16)
            for u in range(2):
                turn_x(0, 0, u)
            turn_back(0, 0)
            pe.wait_ge(weights_in, 16 * N_LOADS)
            pe.wait_ge(weights_by_pool, 16 * N_POOL_LOADS)
            pe.transpose(bG[0:C, C:P], w_nat[0:C, 3, 0:C], eye[0:C, 0:C])
            pe.matmul(bF[:, 0:E // 2 * C], centre, ew_nat[:, :, :].rearrange("p a c -> p (a c)"), start=True, stop=True)
            pe.matmul(bA[:, 0:P], bias_rows, eb_in[:, :], start=True, stop=True)
            pe.matmul(bA[:, P:2 * P], centre, rw_nat[:, :], start=True, stop=True)
            pe.wait_ge(set_dve, N_SET_KQ)
            pe.transpose(bH[:, 0:P], w_cen[:, 0, :], eye)
            pe.transpose(bH[:, P:2 * P], w_cen[:, 1, :], eye).then_inc(set_pe, 1)
            pe.wait_ge(set_dve, N_SET_V)
            pe.transpose(bG[:, 0:C], w_cen[0:C, 2, :], eye[0:C, 0:C]).then_inc(set_pe, 1)
            pe.wait_ge(bias_spread, 3)
            pe.wait_ge(set_dve, N_SET_KEYS)
            with pe.Fori(0, BATCH - 1) as b:
                batch(b, True)
            batch(BATCH - 1, False)


_INS = ['x', 'L0_conv_Wk', 'L0_conv_bk', 'L0_conv_Wq', 'L0_conv_bq', 'L0_conv_Wv', 'L0_conv_bv', 'L0_conv_Wr',
        'L0_conv_br', 'L0_ffn_router_w', 'L0_ffn_router_b', 'L0_ffn_expert_w', 'L0_ffn_expert_b']
_OUTS = [((BATCH, C, 128, 128), 'float32')]


def kernel(**inputs):
    import numpy as _np
    import concourse.bacc as _bacc
    from concourse import mybir as _mybir
    from concourse.bass_utils import run_bass_kernel_spmd as _run

    nc = _bacc.Bacc("TRN2", target_bir_lowering=False, num_devices=1)
    arrays, args = {}, []
    const = dict(zip(("const32", "const_sel", "const_eye"), constants()))
    for name, a in [(n, inputs[n]) for n in _INS] + list(const.items()):
        a = _np.ascontiguousarray(a)
        arrays[f"in_{name}_dram"] = a
        args.append(nc.dram_tensor(f"in_{name}_dram", a.shape, _mybir.dt.from_np(a.dtype), kind="ExternalInput").ap())
    for i, (shape, dtype) in enumerate(_OUTS):
        dt = _mybir.dt.from_np(_np.dtype(dtype))
        args.append(nc.dram_tensor(f"out_{i}_dram", shape, dt, kind="ExternalOutput").ap())
    metaformer_block(nc, *args)
    r = _run(nc, [arrays], core_ids=[0])
    got = tuple(r.results[0][f"out_{i}_dram"] for i in range(len(_OUTS)))
    return got[0]
```
